# Optimizing a Trainium2 kernel written in Bass

```python
import numpy as np
import jax
import jax.numpy as jnp

def _softmax(x, axis=-1):
    return jax.nn.softmax(x, axis=axis)

def _gelu(x):
    return jax.nn.gelu(x, approximate=True)

def _silu(x):
    return jax.nn.silu(x)

def _sigmoid(x):
    return jax.nn.sigmoid(x)

def _layernorm(x, axis=-1, eps=1e-05):
    m = jnp.mean(x, axis=axis, keepdims=True)
    v = jnp.var(x, axis=axis, keepdims=True)
    return (x - m) / jnp.sqrt(v + eps)

def _scatter_add(tgt, idx, src, axis=0):
    return tgt.at[idx].add(src)

def _segment_sum(src, seg, n):
    return jax.ops.segment_sum(src, seg, n)
kernel_name = 'mk_decoder_postln_d1_seqx_r4_f1f54d'

def setup_inputs(seed: int=0):
    np.random.seed(seed)
    _w = jnp.asarray

    def _rec_inputs():
        import jax
        import jax.numpy as jnp
        _rk = jax.random.key(seed)
        x = -0.000125 + 0.9999 * jax.random.normal(jax.random.fold_in(_rk, 1), (2, 512, 1024), jnp.float32)
        _lenS = 512 - jax.random.randint(jax.random.fold_in(_rk, 7), (2,), 0, max(1, 512 // 4) + 1, jnp.int32)
        _lenS2 = 1024 - jax.random.randint(jax.random.fold_in(_rk, 8), (2,), 0, max(1, 1024 // 4) + 1, jnp.int32)
        _ctx_4096P = jax.random.normal(jax.random.fold_in(_rk, 11), (2, 16, 1024), jnp.float32)
        _ctx_4096c = jax.random.dirichlet(jax.random.fold_in(_rk, 511), 0.3 * jnp.ones((16,), jnp.float32), (2, 1024))
        _ctx_4096t = jnp.einsum('bsk,bkd->bsd', _ctx_4096c, _ctx_4096P)
        _ctx_4096t = _ctx_4096t * jax.lax.rsqrt(jnp.mean(jnp.square(_ctx_4096t)) + 1e-12) * 0.953939
        ctx_4096 = -5.72187e-05 + 0.999849 * (_ctx_4096t + 0.3 * jax.random.normal(jax.random.fold_in(_rk, 611), (2, 1024, 1024), jnp.float32))
        return (x, ctx_4096)
    x, ctx_4096 = _rec_inputs()

    def _L0_attn_setup():
        import jax, jax.numpy as jnp
        import numpy as np
        BATCH, SEQ, HIDDEN = (2, 1024, 1024)
        HEADS, HEAD_DIM, BLOCK = (32, 128, 64)
        LAYER_IDX, N_LAYERS = (1, 32)
        EPS = 1e-05

        def _decays():
            base = 1.0 / 2.0 ** (8.0 / HEADS)
            exponent = jnp.arange(HEADS, dtype=jnp.float32) + 1.0
            factor = 1.0 - LAYER_IDX / (N_LAYERS - 1 + 1e-05) + 1e-05
            slope = (base ** exponent * factor)[:, None, None]
            r = jnp.arange(BLOCK, dtype=jnp.float32) + 1.0
            q_decay = jnp.exp(-slope * r[:, None])
            k_decay = jnp.exp(-slope * (BLOCK - r)[:, None])
            diff = r[:, None] - r[None, :]
            diag = slope[None] * diff[None, None]
            diag = jnp.where(diag >= 0, -diag, -jnp.inf)
            diag_decay = jnp.exp(diag)
            block_decay = jnp.exp(-slope * BLOCK)
            return (q_decay, k_decay, diag_decay, block_decay)
        key = jax.random.key(seed)
        ks = jax.random.split(key, 5)
        s = 0.02
        return {'hidden_states': jax.random.normal(ks[0], (BATCH, SEQ, HIDDEN), jnp.float32), 'qkv_w': jax.random.normal(ks[1], (3 * HEADS * HEAD_DIM, HIDDEN), jnp.float32) * s, 'out_w': jax.random.normal(ks[2], (HIDDEN, HEADS * HEAD_DIM), jnp.float32) * s, 'gate_w': jax.random.normal(ks[3], (HEADS * HEAD_DIM, HIDDEN), jnp.float32) * s, 'norm_w': jnp.ones((HEADS * HEAD_DIM,), jnp.float32)}
    _L0_attn_all = _L0_attn_setup()
    _L0_attn_in = {k: v for k, v in _L0_attn_all.items() if k in ('qkv_w', 'out_w', 'gate_w', 'norm_w')}
    del _L0_attn_all

    def _L0_xattn_setup():
        import jax, jax.numpy as jnp
        import numpy as np
        QMIN = 0.0
        QMAX = 255.0

        def fake_quant(x, scale, zp):
            s = scale.reshape(())
            z = zp.reshape(())
            q = jnp.clip(jnp.round(x / s + z), QMIN, QMAX)
            return (q - z) * s
        key = jax.random.key(seed)
        k1, k2 = jax.random.split(key)
        B, M, K, N = (4, 512, 1024, 1024)
        x1 = jax.random.normal(k1, (B, M, K), dtype=jnp.float32)
        x2 = jax.random.normal(k2, (B, K, N), dtype=jnp.float32)
        x1_scale = jnp.full((1,), 8.0 / 255.0, dtype=jnp.float32)
        x1_zp = jnp.full((1,), 128.0, dtype=jnp.float32)
        x2_scale = jnp.full((1,), 8.0 / 255.0, dtype=jnp.float32)
        x2_zp = jnp.full((1,), 128.0, dtype=jnp.float32)
        return {'x1': x1, 'x2': x2, 'x1_scale': x1_scale, 'x1_zp': x1_zp, 'x2_scale': x2_scale, 'x2_zp': x2_zp}
    _L0_xattn_all = _L0_xattn_setup()
    _L0_xattn_in = {k: v for k, v in _L0_xattn_all.items() if k in ('x1_scale', 'x1_zp', 'x2_scale', 'x2_zp')}
    del _L0_xattn_all

    def _L0_ffn_setup():
        import jax, jax.numpy as jnp
        import numpy as np
        B, L, H, Dh, M = (4, 512, 16, 64, 256)
        D = H * Dh
        key = jax.random.key(seed)
        kx, ku, kd, kp = jax.random.split(key, 4)
        x = jax.random.normal(kx, (B, L, D), dtype=jnp.float32)
        up = jax.random.normal(ku, (H, Dh, M), dtype=jnp.float32)
        down = jax.random.normal(kd, (H, M, Dh), dtype=jnp.float32)
        perm = jax.random.permutation(kp, D)
        return {'x': x, 'up': up, 'down': down, 'perm': perm}
    _L0_ffn_all = _L0_ffn_setup()
    _L0_ffn_in = {k: v for k, v in _L0_ffn_all.items() if k in ('up', 'down', 'perm')}
    del _L0_ffn_all
    return {'x': x, 'ctx_4096': ctx_4096, 'L0_attn_qkv_w': _L0_attn_in['qkv_w'], 'L0_attn_out_w': _L0_attn_in['out_w'], 'L0_attn_gate_w': _L0_attn_in['gate_w'], 'L0_attn_norm_w': _L0_attn_in['norm_w'], 'L0_xattn_x1_scale': _L0_xattn_in['x1_scale'], 'L0_xattn_x1_zp': _L0_xattn_in['x1_zp'], 'L0_xattn_x2_scale': _L0_xattn_in['x2_scale'], 'L0_xattn_x2_zp': _L0_xattn_in['x2_zp'], 'L0_ffn_up': _L0_ffn_in['up'], 'L0_ffn_down': _L0_ffn_in['down'], 'L0_ffn_perm': _L0_ffn_in['perm']}

def reference(x, ctx_4096, L0_attn_qkv_w, L0_attn_out_w, L0_attn_gate_w, L0_attn_norm_w, L0_xattn_x1_scale, L0_xattn_x1_zp, L0_xattn_x2_scale, L0_xattn_x2_zp, L0_ffn_up, L0_ffn_down, L0_ffn_perm):
    import jax
    import jax.numpy as jnp

    def _L0_attn_ref(hidden_states, qkv_w, out_w, gate_w, norm_w):
        import jax, jax.numpy as jnp
        import numpy as np
        BATCH, SEQ, HIDDEN = (2, 1024, 1024)
        HEADS, HEAD_DIM, BLOCK = (32, 128, 64)
        LAYER_IDX, N_LAYERS = (1, 32)
        EPS = 1e-05

        def _decays():
            base = 1.0 / 2.0 ** (8.0 / HEADS)
            exponent = jnp.arange(HEADS, dtype=jnp.float32) + 1.0
            factor = 1.0 - LAYER_IDX / (N_LAYERS - 1 + 1e-05) + 1e-05
            slope = (base ** exponent * factor)[:, None, None]
            r = jnp.arange(BLOCK, dtype=jnp.float32) + 1.0
            q_decay = jnp.exp(-slope * r[:, None])
            k_decay = jnp.exp(-slope * (BLOCK - r)[:, None])
            diff = r[:, None] - r[None, :]
            diag = slope[None] * diff[None, None]
            diag = jnp.where(diag >= 0, -diag, -jnp.inf)
            diag_decay = jnp.exp(diag)
            block_decay = jnp.exp(-slope * BLOCK)
            return (q_decay, k_decay, diag_decay, block_decay)
        b, s, _ = hidden_states.shape
        h, d, bs = (HEADS, HEAD_DIM, BLOCK)
        nb = s // bs
        q_decay, k_decay, diag_decay, block_decay = _decays()
        qkv = jax.nn.silu(hidden_states @ qkv_w.T)
        qkv = qkv.reshape(b, s, h, 3, d)
        q = jnp.moveaxis(qkv[:, :, :, 0], 2, 1)
        k = jnp.moveaxis(qkv[:, :, :, 1], 2, 1)
        v = jnp.moveaxis(qkv[:, :, :, 2], 2, 1)

        def to_blocks(x):
            return jnp.moveaxis(x.reshape(b, h, nb, bs, d), 2, 0)
        qb, kb, vb = (to_blocks(q), to_blocks(k), to_blocks(v))

        def step(kv, blk):
            cq, ck, cv = blk
            scores = jnp.einsum('bhnd,bhmd->bhnm', cq, ck) * diag_decay
            intra = jnp.einsum('bhnm,bhmd->bhnd', scores, cv)
            inter = jnp.einsum('bhnd,bhde->bhne', cq * q_decay, kv)
            kv_next = kv * block_decay + jnp.einsum('bhnd,bhne->bhde', ck * k_decay, cv)
            return (kv_next, intra + inter)
        kv0 = jnp.zeros((b, h, d, d), hidden_states.dtype)
        _, out_blocks = jax.lax.scan(step, kv0, (qb, kb, vb))
        attn = jnp.moveaxis(out_blocks, 0, 2)
        attn = attn.reshape(b, h, s, d).transpose(0, 2, 1, 3).reshape(b, s, h * d)
        xf = attn.astype(jnp.float32)
        xf = xf * jax.lax.rsqrt(jnp.mean(xf * xf, axis=-1, keepdims=True) + EPS)
        normed = norm_w * xf.astype(attn.dtype)
        gate = jax.nn.sigmoid(hidden_states @ gate_w.T)
        return gate * normed @ out_w.T

    def _L0_xattn_ref(x1, x2, x1_scale, x1_zp, x2_scale, x2_zp):
        import jax, jax.numpy as jnp
        import numpy as np
        QMIN = 0.0
        QMAX = 255.0

        def fake_quant(x, scale, zp):
            s = scale.reshape(())
            z = zp.reshape(())
            q = jnp.clip(jnp.round(x / s + z), QMIN, QMAX)
            return (q - z) * s
        q1 = fake_quant(x1, x1_scale, x1_zp)
        q2 = fake_quant(x2, x2_scale, x2_zp)
        return jnp.matmul(q1, q2)

    def _L0_ffn_ref(x, up, down, perm):
        import jax, jax.numpy as jnp
        import numpy as np
        B, L, H, Dh, M = (4, 512, 16, 64, 256)
        D = H * Dh
        b, l, Dm = x.shape
        h, d = (up.shape[0], up.shape[1])
        unperm = jnp.argsort(perm)
        t = x.reshape(b * l, Dm)
        t = t[:, perm]
        t = t.reshape(b * l, h, d)
        t = jnp.einsum('bhd,hdm->bhm', t, up)
        t = jax.nn.gelu(t, approximate=False)
        t = jnp.einsum('bhm,hmd->bhd', t, down)
        t = t.reshape(b * l, h * d)
        t = t[:, unperm]
        out = t.reshape(b, l, Dm)
        return out
    x = _layernorm(x + _L0_attn_ref(x, L0_attn_qkv_w, L0_attn_out_w, L0_attn_gate_w, L0_attn_norm_w), axis=-1)
    x = _layernorm(x + _L0_xattn_ref(x, ctx_4096, L0_xattn_x1_scale, L0_xattn_x1_zp, L0_xattn_x2_scale, L0_xattn_x2_zp), axis=-1)
    x = _layernorm(x + _L0_ffn_ref(x, L0_ffn_up, L0_ffn_down, L0_ffn_perm), axis=-1)
    return x

_drawn_inputs = setup_inputs


def setup_inputs(seed=0):
    import zlib

    import numpy as np

    out = dict(_drawn_inputs(seed))
    spreads = {'L0_attn_norm_w': (1.0, 0.2)}
    factors = {}
    for name, (base, spread) in spreads.items():
        noise = np.random.default_rng([zlib.crc32(name.encode()), seed]).standard_normal(out[name].shape)
        drawn = base * np.exp(spread * noise) if base else spread * noise
        out[name] = jnp.asarray(drawn.astype(out[name].dtype))
    for name, factor in factors.items():
        out[name] = (out[name] * factor).astype(out[name].dtype)
    return out
```

```python
import concourse.bass as bass
from concourse import mybir
from contextlib import ExitStack

F32 = mybir.dt.float32
F16 = mybir.dt.float16
BF16 = mybir.dt.bfloat16
I32 = mybir.dt.int32
ALU = mybir.AluOpType
ACT = mybir.ActivationFunctionType

P = 128
B, S, D = 2, 512, 1024
KT = D // P
ST = S // P
H, HD = 32, 128
GH = 2
NG = H // GH
CTX = 1024
FH, FD, FM = 16, 64, 256
FP = FH * FD // P
HALF = 512
W_SCALE = 64.0
G_SCALE = 1.0 / 16.0
EPS = 1e-5
Q_MAX = 255.0
Q_MID = 128.0
ROUND = 1.5 * 2.0 ** 23
LAYER_IDX, N_LAYERS = 1, 32


class Event:

    def __init__(self, sem):
        self.sem, self.count = sem, 0


class Stream:

    def __init__(self, engine):
        self.engine, self.met = engine, {}

    def wait(self, *tokens):
        for token in tokens:
            if token is None:
                continue
            event, value = token
            if self.met.get(event, 0) < value:
                self.met[event] = value
                self.engine.wait_ge(event.sem, value)

    def do(self, fn, signal=None, by=1):
        ins = fn(self.engine)
        if signal is None:
            return None
        ins.then_inc(signal.sem, by)
        signal.count += by
        return signal, signal.count


class Banks:

    def __init__(self, banks):
        self.banks, self.free, self.at = banks, [None] * len(banks), 0

    def take(self):
        i, self.at = self.at, (self.at + 1) % len(self.banks)
        return i, self.banks[i], self.free[i]


def decoder_program(nc, x_t, x_n, w_qk, w_v, w_gate, w_out, norm_w, decay, ident, ctx_in, quant, up, down,
                    perm, out_b, scratch_b):
    stack = ExitStack()
    with stack:
        def sb(name, shape, dt):
            return stack.enter_context(nc.sbuf_tensor(name, shape, dt))

        def event(name):
            return Event(stack.enter_context(nc.semaphore(name)))

        stage_x = [sb(f"x_split{b}", [P, 2, KT, S], F16) for b in range(B)]
        x_hl = [t[:, :, :, :] for t in stage_x]
        ctx_q = [t[:, :, :, :].rearrange("p a k n -> p (a k n)").bitcast(BF16)
                  .rearrange("p (k n) -> p k n", k=KT) for t in stage_x]
        acc = [sb(f"acc{b}", [P, ST, D], F32) for b in range(B)]
        x2p = [a[:, :, :].rearrange("p t d -> p (t d)").rearrange("p (k s) -> p k s", k=KT) for a in acc]
        w_head = [sb(f"w_head{i}", [P, 3, 2, KT, P], F16) for i in range(2)]
        w_vg = sb("w_v_group", [P, 2, KT, GH * HD], F16)
        w_og = sb("w_out_group", [P, GH, 2, D], F16)
        NSTAGE = 3
        raw = [sb(f"raw{i}", [P, D], F32) for i in range(NSTAGE)]
        decay_sb = [sb(f"decay{i}", [P, S], F32) for i in range(2)]
        q_hl = sb("q_split", [P, 2, S], F16)
        k_hl = sb("k_split", [P, 2, S], F16)
        v_hl = sb("v_split", [P, B, 2, ST, GH * HD], F16)
        silu32 = [sb(f"silu32_{i}", [P, S], F32) for i in range(3)]
        sig32 = [sb(f"sig32_{i}", [P, S], F32) for i in range(2)]
        gate32 = [sb(f"gate32_{i}", [P, S], F32) for i in range(2)]
        NS = sum(S - P * j for j in range(ST))
        s32 = sb("scores32", [P, NS], F32)
        s_hl = sb("scores_split", [P, 2, NS], F16)
        g32 = sb("gated32", [P, S], F32)
        g_hl = sb("gated_split", [P, GH, B, 2, S], F16)
        sq32 = sb("square32", [P, S], F32)
        ssq = sb("ssq", [P, B, S], F32)
        nw_sb = sb("norm_w_sb", [P, H], F32)
        ident32 = sb("ident32", [P, P], F32)
        ident16 = sb("ident16", [P, P], BF16)
        ones32 = sb("ones32", [P, P], F32)
        ones16 = sb("ones16", [P, P], BF16)
        perm_sb = sb("perm_sb", [P, KT], I32)
        quant_sb = sb("quant_sb", [P, 4], F32)
        qc = sb("quant_consts", [P, 12], F32)
        eps_sb = sb("eps_sb", [P, 2], F32)
        up_hl = sb("up_split", [P, 2, FP, FM], F16)
        down_hl = sb("down_split", [P, 2, FH * 2, FD], F16)
        q1_n = sb("q1_n", [P, D], BF16)
        q1_t = sb("q1_t", [P, KT, P], BF16)
        ctx_row = sb("ctx_row", [P, D], F32)
        stats = sb("stats", [P, 2, 6], F32)
        small = sb("small", [P, 16], F32)
        h32 = [silu32[0], silu32[1]]
        h_hl = [sb(f"h_split{i}", [P, 2, S], F16) for i in range(4)]
        mean_b = gate32[0]
        rstd_b = gate32[1]

        banks = [stack.enter_context(nc.psum_tensor(f"bank{i}", [P, HALF], F32)) for i in range(8)]
        ring = Banks(banks[0:4])
        sring = Banks(banks[4:7])
        av_bank = banks[7]

        raw_in = [event(f"raw_in{i}") for i in range(NSTAGE)]
        decay_in = [event(f"decay_in{i}") for i in range(2)]
        const_in = event("const_in")
        pe = event("pe_done")
        act = event("act_done")
        dve = event("dve_done")
        pool = event("pool_done")
        raw_out = [event(f"raw_out{i}") for i in range(NSTAGE)]
        gathered = event("gathered")
        stored = event("stored")

        SP, PE, AC, DV, PL = (Stream(e) for e in (nc.sync, nc.tensor, nc.scalar, nc.vector, nc.gpsimd))

        raw_free = [None] * NSTAGE
        raw_at = [0]

        def load(src, n=D):
            i = raw_at[0] % NSTAGE
            raw_at[0] += 1
            SP.wait(*(raw_free[i] or ()))
            t = SP.do(lambda e: e.dma_start(raw[i][:, 0:n], src), raw_in[i], 16)
            return i, t

        def split(src, n, scale, hi, lo, ready, dst_free, shape=None):
            view = src if shape is None else shape(src)
            AC.wait(*ready, *dst_free)
            t_hi = AC.do(lambda e: e.activation(hi, view, ACT.Copy, scale=scale), act)
            DV.wait(*ready, t_hi)
            t_lo = DV.do(lambda e: e.scalar_tensor_tensor(out=lo, in0=view, scalar=scale, in1=hi,
                                                          op0=ALU.mult, op1=ALU.subtract), dve)
            return t_hi, t_lo

        def load_split(src, n, scale, hi, lo, dst_free=()):
            i, t = load(src, n)
            t_hi, t_lo = split(raw[i][:, 0:n], n, scale, hi, lo, [t], dst_free)
            raw_free[i] = (t_lo,)
            return t_lo

        for dst, src in ((nw_sb, norm_w), (ident32, ident), (perm_sb, perm), (quant_sb, quant)):
            t_const = SP.do(lambda e, dst=dst, src=src: e.dma_start(dst[:, :], src), const_in, 16)
        DV.do(lambda e: e.memset(ones32[:, :], 1.0), dve)
        DV.do(lambda e: e.memset(ones16[:, :], 1.0), dve)
        DV.do(lambda e: e.memset(eps_sb[:, 0:1], EPS), dve)
        DV.do(lambda e: e.memset(eps_sb[:, 1:2], EPS / (G_SCALE * W_SCALE) ** -2), dve)
        t_ones = DV.do(lambda e: e.memset(ssq[:, :, :], 0.0), dve)
        DV.wait(t_const)
        t_ident = DV.do(lambda e: e.tensor_copy(ident16[:, :], ident32[:, :]), dve)
        (S1, Z1, S2, Z2) = (quant_sb[:, i:i + 1] for i in range(4))
        INV1, INV2, C1, C2, S12, C1S, C2S, KC = (qc[:, i:i + 1] for i in range(8))

        def dchain(fn):
            t = DV.do(fn, dve)
            DV.wait(t)
            return t

        DV.wait(t_ident)
        dchain(lambda e: e.reciprocal(INV1, S1))
        dchain(lambda e: e.reciprocal(INV2, S2))
        dchain(lambda e: e.tensor_scalar(C1, Z1, -1.0, Q_MID, ALU.mult, ALU.add))
        dchain(lambda e: e.tensor_scalar(C2, Z2, -1.0, Q_MID, ALU.mult, ALU.add))
        dchain(lambda e: e.tensor_tensor(S12, S1, S2, ALU.mult))
        dchain(lambda e: e.tensor_tensor(C1S, C1, S12, ALU.mult))
        dchain(lambda e: e.tensor_tensor(C2S, C2, S12, ALU.mult))
        dchain(lambda e: e.tensor_tensor(KC, C1S, C2, ALU.mult))
        t_qc = dchain(lambda e: e.tensor_scalar(KC, KC, float(CTX), None, ALU.mult))

        head_ready, head_free = {}, {0: (), 1: ()}
        v_ready, v_free = {}, []
        o_ready, o_free = {}, []
        decay_ready, decay_free = {}, {0: (), 1: ()}

        def prefetch_head(h):
            slot = h % 2
            wt = w_head[slot]
            tokens = []
            for c, src in ((0, w_qk[h, 0]), (1, w_qk[h, 1]), (2, w_gate[h])):
                hi = wt[:, c, 0].rearrange("p k m -> p (k m)")
                lo = wt[:, c, 1].rearrange("p k m -> p (k m)")
                tokens.append(load_split(src, D, W_SCALE, hi, lo, head_free[slot]))
            head_ready[h] = tokens
            SP.wait(*decay_free[slot])
            decay_ready[h] = SP.do(lambda e: e.dma_start(decay_sb[slot][:, :], decay[h]), decay_in[slot], 16)

        def prefetch_v(g):
            half = KT // 2
            tokens = []
            for i in range(2):
                src = w_v[g, :, i * half * GH * HD:(i + 1) * half * GH * HD]
                hi = w_vg[:, 0, i * half:(i + 1) * half].rearrange("p k m -> p (k m)")
                lo = w_vg[:, 1, i * half:(i + 1) * half].rearrange("p k m -> p (k m)")
                tokens.append(load_split(src, D, W_SCALE, hi, lo, v_free))
            v_ready[g] = tokens

        def prefetch_o(g):
            o_ready[g] = [load_split(w_out[g * GH + i], D, W_SCALE, w_og[:, i, 0, :], w_og[:, i, 1, :], o_free)
                          for i in range(GH)]

        def three(out, pairs, signal=True):
            n = 3 * len(pairs)
            m = 0
            for (a_hi, a_lo), (b_hi, b_lo) in pairs:
                for a, b_ in ((a_hi, b_hi), (a_hi, b_lo), (a_lo, b_hi)):
                    m += 1
                    t = PE.do(lambda e, a=a, b_=b_, m=m: e.matmul(out, a, b_, start=m == 1, stop=m == n),
                              pe if (m == n and signal) else None)
            return t

        silu_at = [0]
        sig_at = [0]
        silu_free = [(), (), ()]
        sig_free = [(), ()]

        def silu_split(bank, t_mm, n, hi, lo, dst_free, shape=lambda a: a):
            si, gi = silu_at[0] % 3, sig_at[0] % 2
            silu_at[0] += 1
            sig_at[0] += 1
            s_, g_ = silu32[si][:, 0:n], sig32[gi][:, 0:n]
            AC.wait(t_mm, *sig_free[gi])
            t_sig = AC.do(lambda e: e.activation(g_, bank[:, 0:n], ACT.Sigmoid, scale=1.0 / W_SCALE), act)
            DV.wait(t_mm, t_sig, *silu_free[si])
            t_s = DV.do(lambda e: e.scalar_tensor_tensor(out=s_, in0=bank[:, 0:n], scalar=1.0 / W_SCALE, in1=g_,
                                                         op0=ALU.mult, op1=ALU.mult), dve)
            sig_free[gi] = (t_s,)
            AC.wait(t_s, *dst_free)
            t_hi = AC.do(lambda e: e.activation(hi, shape(s_), ACT.Copy), act)
            DV.wait(t_hi)
            t_lo = DV.do(lambda e: e.tensor_tensor(lo, shape(s_), hi, ALU.subtract), dve)
            silu_free[si] = (t_lo,)
            return t_s, (t_hi, t_lo)

        x_ready = []

        def load_x():
            for k in range(KT):
                i, t = load(x_t[:, k, :])
                toks = []
                for b in range(B):
                    _, t_lo = split(raw[i][:, b * S:(b + 1) * S], S, 1.0, x_hl[b][:, 0, k], x_hl[b][:, 1, k], [t], ())
                    toks.append(t_lo)
                raw_free[i] = (toks[-1],)
                x_ready.append(toks)

        state = {"q": (), "k": (), "qk_free": (), "gate": {}, "gate_free": [(), ()], "v": {}, "v_free": (),
                 "s": (), "s32_free": (), "s_free": (), "g": {}, "g_free": (), "sq": (), "ssq": t_ones, "acc": {},
                 "g32_free": (), "sq_free": ()}
        av_free = []
        x_last_read = [None, None]

        def project(h, b, c):
            i, bank, free = ring.take()
            PE.wait(free, *head_ready[h])
            PE.wait(x_ready[-1][b])
            wt = w_head[h % 2]
            t = three(bank[:, :], [((wt[:, c, 0, k], wt[:, c, 1, k]), (x_hl[b][:, 0, k], x_hl[b][:, 1, k]))
                                   for k in range(KT)])
            if c == 2:
                slot = (h * B + b) % 2
                g_ = gate32[slot]
                AC.wait(t, *state["gate_free"][slot])
                t_g = AC.do(lambda e: e.activation(g_[:, :], bank[:, :], ACT.Sigmoid, scale=1.0 / W_SCALE), act)
                state["gate"][(h, b)] = (slot, t_g)
                ring.free[i] = t_g
                head_free[h % 2] = (t,)
                x_last_read[b] = t
            else:
                dst = (q_hl, k_hl)[c]
                t_free, ready = silu_split(bank, t, S, dst[:, 0], dst[:, 1], state["qk_free"])
                ring.free[i] = t_free
                state["qk"[c]] = ready

        def project_v(g):
            for b in range(B):
                for s in range(ST):
                    i, bank, free = ring.take()
                    PE.wait(free, *v_ready[g])
                    PE.wait(x_ready[-1][b])
                    cols = slice(s * P, (s + 1) * P)
                    t = three(bank[:, 0:GH * HD],
                              [((x_hl[b][:, 0, k, cols], x_hl[b][:, 1, k, cols]), (w_vg[:, 0, k], w_vg[:, 1, k]))
                               for k in range(KT)])
                    t_free, ready = silu_split(bank, t, GH * HD, v_hl[:, b, 0, s], v_hl[:, b, 1, s], state["v_free"])
                    ring.free[i] = t_free
                    state["v"][(g, b)] = ready
            v_free[:] = [t]

        offs = [sum(S - P * i for i in range(j)) for j in range(ST)]

        def scores(h, b):
            ia, bank_a, free_a = sring.take()
            ib, bank_b, free_b = sring.take()
            ic, bank_c, free_c = sring.take()
            PE.wait(free_a, free_b, free_c, *state["q"], *state["k"])
            places = {0: bank_a[:, 0:S], 1: bank_b[:, 0:S - P], 2: bank_c[:, 0:S - 2 * P], 3: bank_b[:, S - P:S]}
            slot = h % 2
            t_last = None
            for group in ((0,), (1, 3), (2,)):
                for j in group:
                    cols, keys = slice(j * P, S), slice(j * P, (j + 1) * P)
                    t = three(places[j], [((k_hl[:, 0, keys], k_hl[:, 1, keys]), (q_hl[:, 0, cols], q_hl[:, 1, cols]))])
                DV.wait(t, decay_ready[h], *state["s32_free"])
                for j in group:
                    n = S - P * j
                    t_last = DV.do(lambda e: e.tensor_tensor(s32[:, offs[j]:offs[j] + n], places[j],
                                                             decay_sb[slot][:, 0:n], ALU.mult), dve)
            state["qk_free"] = (t,)
            sring.free[ia] = sring.free[ib] = sring.free[ic] = t_last
            decay_free[slot] = (t_last,)
            AC.wait(t_last, *state["s_free"])
            t_hi = AC.do(lambda e: e.activation(s_hl[:, 0, :], s32[:, :], ACT.Copy), act)
            DV.wait(t_hi)
            t_lo = DV.do(lambda e: e.tensor_tensor(s_hl[:, 1, :], s32[:, :], s_hl[:, 0, :], ALU.subtract), dve)
            state["s32_free"] = (t_lo,)
            state["s"] = (t_hi, t_lo)

        def attend(h, b):
            g, hh = h // GH, h % GH
            PE.wait(*av_free, *state["s"], *state["v"][(g, b)])
            out = av_bank
            n_mm = 3 * ST
            m = 0
            for j in range(ST):
                n = S - P * j
                cols = slice(hh * HD, (hh + 1) * HD)
                vh, vl = v_hl[:, b, 0, j, cols], v_hl[:, b, 1, j, cols]
                sh, sl = s_hl[:, 0, offs[j]:offs[j] + n], s_hl[:, 1, offs[j]:offs[j] + n]
                for a, b_ in ((vh, sh), (vh, sl), (vl, sh)):
                    m += 1
                    t = PE.do(lambda e, a=a, b_=b_, m=m, j=j: e.matmul(out[:, j * P:S], a, b_, start=m == 1,
                                                                       stop=m == n_mm), pe if m == n_mm else None)
            state["s_free"] = (t,)
            state["v_free"] = (t,)
            slot, t_gate = state["gate"].pop((h, b))
            AC.wait(t, *state["sq_free"])
            t_sq = AC.do(lambda e: e.activation(sq32[:, :], out[:, :], ACT.Square), act)
            DV.wait(t_sq, t_gate, *state["g32_free"])
            t_g = DV.do(lambda e: e.scalar_tensor_tensor(out=g32[:, :], in0=out[:, :], scalar=nw_sb[:, h:h + 1],
                                                         in1=gate32[slot][:, :], op0=ALU.mult, op1=ALU.mult), dve)
            state["gate_free"][slot] = (t_g,)
            av_free[:] = [t_g]
            DV.wait(t_sq, state["ssq"])
            t_ssq = DV.do(lambda e: e.tensor_tensor(ssq[:, b], ssq[:, b], sq32[:, :], ALU.add), dve)
            state["ssq"] = t_ssq
            state["sq_free"] = (t_ssq,)
            ready = split(g32[:, :], S, G_SCALE, g_hl[:, hh, b, 0], g_hl[:, hh, b, 1], [t_g], state["g_free"])
            state["g32_free"] = (ready[1],)
            state["g"][(h, b)] = ready

        def out_product(g, b):
            ready = [t for i in range(GH) for t in state["g"].pop((g * GH + i, b))]
            for s in range(ST):
                for half in range(2):
                    i, bank, free = ring.take()
                    PE.wait(free, *o_ready[g], *ready)
                    cols, outs = slice(s * P, (s + 1) * P), slice(half * HALF, (half + 1) * HALF)
                    t = three(bank[:, :], [((g_hl[:, a, b, 0, cols], g_hl[:, a, b, 1, cols]),
                                            (w_og[:, a, 0, outs], w_og[:, a, 1, outs])) for a in range(GH)])
                    dst = acc[b][:, s, outs]
                    DV.wait(t)
                    if g == 0:
                        t_acc = DV.do(lambda e, dst=dst, bank=bank: e.tensor_copy(dst, bank[:, :]), dve)
                    else:
                        DV.wait(state["acc"][(b, s, half)])
                        t_acc = DV.do(lambda e, dst=dst, bank=bank: e.tensor_tensor(dst, dst, bank[:, :], ALU.add), dve)
                    state["acc"][(b, s, half)] = t_acc
                    ring.free[i] = t_acc
            state["g_free"] = (t,)
            o_free[:] = [t]

        def load_ffn_weights():
            up_ready = []
            for i in range(2):
                n = FP * FM // 2
                sl = slice(i * n, (i + 1) * n)
                hi = up_hl[:, 0].rearrange("p a m -> p (a m)")[:, sl]
                lo = up_hl[:, 1].rearrange("p a m -> p (a m)")[:, sl]
                up_ready.append(load_split(up[:, sl], n, 1.0, hi, lo))
                n = FH * 2 * FD // 2
                sl = slice(i * n, (i + 1) * n)
                hi = down_hl[:, 0].rearrange("p a m -> p (a m)")[:, sl]
                lo = down_hl[:, 1].rearrange("p a m -> p (a m)")[:, sl]
                up_ready.append(load_split(down[:, sl], n, 1.0, hi, lo))
            return up_ready

        def quantise(dst, src, inv, zero, ready, dst_free):
            DV.wait(*ready)
            t = DV.do(lambda e: e.tensor_scalar(src, src, inv, zero, ALU.mult, ALU.add), dve)
            DV.wait(t)
            t = DV.do(lambda e: e.tensor_scalar(src, src, 0.0, Q_MAX, ALU.max, ALU.min), dve)
            DV.wait(t, *dst_free)
            return DV.do(lambda e: e.tensor_scalar(dst, src, ROUND, ROUND + Q_MID, ALU.add, ALU.subtract), dve)

        ctx_ready = {}
        row_free = [()]

        def quantise_ctx(b):
            toks = []
            for k in range(KT):
                i, t = load(ctx_in[b, k])
                t_q = quantise(ctx_q[b][:, k, :], raw[i][:, :], INV2, Z2, [t, t_qc], [x_last_read[b]])
                raw_free[i] = (t_q,)
                toks.append(t_q)
            ctx_ready[b] = toks[-1]
            for half in range(2):
                outs = slice(half * HALF, (half + 1) * HALF)
                i, bank, free = ring.take()
                PE.wait(free, t_ident, toks[-1])
                for k in range(KT):
                    t = PE.do(lambda e, k=k, bank=bank, outs=outs: e.matmul(
                        bank[:, :], ones16[:, :], ctx_q[b][:, k, outs], start=k == 0, stop=k == KT - 1),
                        pe if k == KT - 1 else None)
                DV.wait(t, *row_free[0])
                t_row = DV.do(lambda e, bank=bank, outs=outs: e.tensor_scalar(
                    ctx_row[:, outs], bank[:, :], C1S, KC, ALU.mult, ALU.add), dve)
                ring.free[i] = t_row
            state["ctx_row"] = t_row

        def norm_tile(x_, ready):
            DV.wait(*ready)
            for i in range(2):
                t = DV.do(lambda e, i=i: e.bn_stats(out=stats[:, i, :], in_=x_[:, i * HALF:(i + 1) * HALF]), dve)
            DV.wait(t)
            t = DV.do(lambda e: e.bn_aggr(out=small[:, 0:2], in_=stats[:, :, :]), dve)
            AC.wait(t)
            t = AC.do(lambda e: e.activation(small[:, 2:3], small[:, 1:2], ACT.Sqrt, bias=eps_sb[:, 0:1]), act)
            DV.wait(t)
            t = DV.do(lambda e: e.reciprocal(small[:, 3:4], small[:, 2:3]), dve)
            DV.wait(t)
            return DV.do(lambda e: e.tensor_scalar(x_, x_, small[:, 0:1], small[:, 3:4], ALU.subtract, ALU.mult), dve)

        q1_free = [()]
        q1t_free = [()]

        def rows_tail(b, s):
            x_ = acc[b][:, s, :]
            i, bank, free = ring.take()
            PE.wait(free, state["ssq"], t_ones)
            t = PE.do(lambda e: e.matmul(bank[:, 0:1], ssq[:, b, s * P:(s + 1) * P], ones32[:, 0:1],
                                         start=True, stop=True), pe)
            up_ = (G_SCALE * W_SCALE) ** 2
            AC.wait(t)
            t_r = AC.do(lambda e: e.activation(small[:, 4:5], bank[:, 0:1], ACT.Sqrt, bias=eps_sb[:, 1:2],
                                               scale=up_ / (H * HD)), act)
            ring.free[i] = t_r
            DV.wait(t_r)
            t = DV.do(lambda e: e.reciprocal(small[:, 5:6], small[:, 4:5]), dve)
            i, t_x = load(x_n[b, s])
            DV.wait(t, t_x, state["acc"][(b, s, 0)], state["acc"][(b, s, 1)])
            t = DV.do(lambda e: e.scalar_tensor_tensor(out=x_, in0=x_, scalar=small[:, 5:6], in1=raw[i][:, :],
                                                       op0=ALU.mult, op1=ALU.add), dve)
            t1 = norm_tile(x_, [t])
            DV.wait(t1)
            t = DV.do(lambda e: e.tensor_scalar(raw[i][:, :], x_, INV1, Z1, ALU.mult, ALU.add), dve)
            DV.wait(t)
            t = DV.do(lambda e: e.tensor_scalar(raw[i][:, :], raw[i][:, :], 0.0, Q_MAX, ALU.max, ALU.min), dve)
            DV.wait(t, *q1_free[0])
            t_q = DV.do(lambda e: e.tensor_scalar(q1_n[:, :], raw[i][:, :], ROUND, ROUND + Q_MID,
                                                  ALU.add, ALU.subtract), dve)
            raw_free[i] = (t_q,)
            i, bank_t, free = ring.take()
            PE.wait(free, t_q, t_ident)
            for k in range(KT):
                t = PE.do(lambda e, k=k: e.transpose(bank_t[:, :].bitcast(BF16)[:, k * P:(k + 1) * P],
                                                     q1_n[:, k * P:(k + 1) * P], ident16[:, :]),
                          pe if k == KT - 1 else None)
            q1_free[0] = (t,)
            AC.wait(t, *q1t_free[0])
            t_q1t = AC.do(lambda e: e.activation(q1_t[:, :, :].rearrange("p k s -> p (k s)"),
                                                 bank_t[:, :].bitcast(BF16), ACT.Copy), act)
            ring.free[i] = t_q1t
            ih = []
            for half in range(2):
                outs = slice(half * HALF, (half + 1) * HALF)
                i, bank, free = ring.take()
                PE.wait(free, t_q1t, ctx_ready[b])
                for k in range(KT):
                    t_mm = PE.do(lambda e, k=k, bank=bank, outs=outs: e.matmul(
                        bank[:, :], q1_t[:, k, :], ctx_q[b][:, k, outs], start=k == 0, stop=k == KT - 1),
                        pe if k == KT - 1 else None)
                ih.append((i, bank, t_mm, outs))
            i, bank_r, free = ring.take()
            PE.wait(free)
            for k in range(KT):
                t = PE.do(lambda e, k=k: e.matmul(bank_r[:, 0:1], q1_t[:, k, :], ones16[:, 0:1], start=k == 0,
                                                  stop=k == KT - 1), pe if k == KT - 1 else None)
            q1t_free[0] = (t,)
            DV.wait(t)
            t = DV.do(lambda e: e.tensor_scalar(small[:, 6:7], bank_r[:, 0:1], C2S, None, ALU.mult), dve)
            ring.free[i] = t
            DV.wait(t, state["ctx_row"])
            t = DV.do(lambda e: e.scalar_tensor_tensor(out=x_, in0=x_, scalar=small[:, 6:7], in1=ctx_row[:, :],
                                                       op0=ALU.add, op1=ALU.add), dve)
            row_free[0] = (t,)
            DV.wait(t)
            for i, bank, t_mm, outs in ih:
                DV.wait(t_mm)
                t = DV.do(lambda e, bank=bank, outs=outs: e.scalar_tensor_tensor(
                    out=x_[:, outs], in0=bank[:, :], scalar=S12, in1=x_[:, outs], op0=ALU.mult, op1=ALU.add), dve)
                ring.free[i] = t
            t2 = norm_tile(x_, [t])
            slot = raw_at[0] % NSTAGE
            raw_at[0] += 1
            for half in range(2):
                i, bank, free = ring.take()
                PE.wait(free, t2)
                for k in range(4):
                    t = PE.do(lambda e, k=k, bank=bank, half=half: e.transpose(
                        bank[:, k * P:(k + 1) * P], x_[:, (half * 4 + k) * P:(half * 4 + k + 1) * P], ident32[:, :]),
                        pe if k == 3 else None)
                AC.wait(t, *(raw_free[slot] or ()))
                t_c = AC.do(lambda e, bank=bank, half=half: e.activation(
                    raw[slot][:, half * HALF:(half + 1) * HALF], bank[:, :], ACT.Copy), act)
                ring.free[i] = t_c
            SP.wait(t_c)
            t_s = SP.do(lambda e: e.dma_start(
                scratch_b[b].rearrange("(k p) s -> p k s", p=P)[:, :, s * P:(s + 1) * P],
                raw[slot][:, :].rearrange("p (k s) -> p k s", k=KT)), raw_out[slot], 16)
            raw_free[slot] = (t_s,)
            return t_s, t

        def ffn_tail(b, t_scratch, t_x2_read, ffn_ready):
            xp = x2p[b]
            PL.wait(*t_scratch, t_const, t_x2_read)
            for k in range(KT):
                t_g = PL.do(lambda e, k=k: e.indirect_dma_start(
                    xp[:, k, :], None, scratch_b[b], bass.IndirectOffsetOnAxis(ap=perm_sb[:, k:k + 1], axis=0)),
                    gathered, 16)
            ready = []
            for k in range(KT):
                ready.append(split(xp[:, k, :], S, 1.0, x_hl[b][:, 0, k], x_hl[b][:, 1, k], [t_g], [ctx_done[0]]))
            h_at = [0]
            h_free = [()] * 4
            h32_free = [(), ()]
            hs = {}

            def up_pair(p):
                PE.wait(*ready[p], *ffn_ready)
                got = []
                for mc in range(2):
                    two = [ring.take() for _ in range(2)]
                    PE.wait(two[0][2], two[1][2])
                    for n, (wi, xi) in enumerate(((0, 0), (0, 1), (1, 0))):
                        for a in range(2):
                            rows = slice(a * FD, (a + 1) * FD)
                            t = PE.do(lambda e, n=n, wi=wi, xi=xi, rows=rows, bank=two[a][1], mc=mc: e.matmul(
                                bank[:, :], up_hl[rows, wi, p, mc * P:(mc + 1) * P], x_hl[b][rows, xi, p, :],
                                start=n == 0, stop=n == 2), pe if n == 2 else None)
                    got += [(a, mc, two[a]) for a in range(2)]
                for a, mc, (i, bank, _) in got:
                    slot, s2 = h_at[0] % 4, h_at[0] % 2
                    h_at[0] += 1
                    AC.wait(t, *h32_free[s2], *h_free[slot])
                    t32 = AC.do(lambda e, bank=bank, s2=s2: e.activation(h32[s2][:, :], bank[:, :], ACT.Gelu), act)
                    t_hi = AC.do(lambda e, bank=bank, slot=slot: e.activation(h_hl[slot][:, 0, :], bank[:, :], ACT.Gelu), act)
                    ring.free[i] = t_hi
                    DV.wait(t_hi)
                    t_lo = DV.do(lambda e, s2=s2, slot=slot: e.tensor_tensor(h_hl[slot][:, 1, :], h32[s2][:, :],
                                                                            h_hl[slot][:, 0, :], ALU.subtract), dve)
                    h32_free[s2] = (t_lo,)
                    hs[(p, a, mc)] = (slot, t_lo)

            sums = {}

            def down_pair(p):
                i, bank, free = sring.take()
                PE.wait(free)
                for mc in range(2):
                    for a in range(2):
                        slot, t_h = hs.pop((p, a, mc))
                        PE.wait(t_h)
                        for n, (wi, hi_) in enumerate(((0, 0), (0, 1), (1, 0))):
                            t = PE.do(lambda e, a=a, mc=mc, n=n, wi=wi, hi_=hi_, slot=slot, bank=bank: e.matmul(
                                bank[a * FD:(a + 1) * FD, :], down_hl[:, wi, (2 * p + a) * 2 + mc, :],
                                h_hl[slot][:, hi_, :], start=mc == 0 and n == 0, stop=mc == 1 and n == 2),
                                pe if n == 2 else None)
                        h_free[slot] = (t,)
                DV.wait(t)
                t = DV.do(lambda e: e.tensor_tensor(xp[:, p, :], bank[:, :], xp[:, p, :], ALU.add), dve)
                sring.free[i] = t
                sums[p] = t

            for p in range(FP):
                up_pair(p)
                down_pair(p)

            def column_sum(tile, tokens):
                i, bank, free = sring.take()
                PE.wait(free)
                for p in range(FP):
                    PE.wait(tokens[p])
                    t = PE.do(lambda e, p=p: e.matmul(bank[:, :], ones32[:, :], tile(p), start=p == 0,
                                                      stop=p == FP - 1), pe if p == FP - 1 else None)
                return i, bank, t

            i, bank, t = column_sum(lambda p: xp[:, p, :], [sums[p] for p in range(FP)])
            AC.wait(t, *state["gate_free"][0])
            t_mean = AC.do(lambda e: e.activation(mean_b[:, :], bank[:, :], ACT.Copy, scale=1.0 / D), act)
            sring.free[i] = t_mean
            centred = []
            for p in range(FP):
                DV.wait(t_mean)
                centred.append(DV.do(lambda e, p=p: e.tensor_tensor(xp[:, p, :], xp[:, p, :], mean_b[:, :],
                                                                    ALU.subtract), dve))
            sq = x_hl[b].rearrange("p a k s -> p (a k s)").bitcast(F32).rearrange("p (k s) -> p k s", k=KT)
            squares = []
            for p in range(FP):
                AC.wait(centred[p], *([pe_last_up[0]] if pe_last_up else []))
                squares.append(AC.do(lambda e, p=p: e.activation(sq[:, p, :], xp[:, p, :], ACT.Square), act))
            i, bank, t = column_sum(lambda p: sq[:, p, :], squares)
            AC.wait(t, *state["gate_free"][1])
            t_sd = AC.do(lambda e: e.activation(rstd_b[:, :], bank[:, :], ACT.Sqrt, bias=eps_sb[:, 0:1],
                                                scale=1.0 / D), act)
            sring.free[i] = t_sd
            DV.wait(t_sd)
            t_rs = DV.do(lambda e: e.reciprocal(rstd_b[:, :], rstd_b[:, :]), dve)
            DV.wait(t_rs)
            for p in range(FP):
                t = DV.do(lambda e, p=p: e.tensor_tensor(xp[:, p, :], xp[:, p, :], rstd_b[:, :], ALU.mult), dve)
                PL.wait(t)
                t_st = PL.do(lambda e, p=p: e.indirect_dma_start(
                    out_b[b], bass.IndirectOffsetOnAxis(ap=perm_sb[:, p:p + 1], axis=0), xp[:, p, :], None),
                    stored, 16)
            state["gate_free"] = [(t,), (t,)]
            return t_st

        pe_last_up = []
        ctx_done = [None]

        load_x()
        prefetch_v(0)
        prefetch_head(0)
        units = []
        for g in range(NG):
            a = [(g, h, b) for h in (g * GH, g * GH + 1) for b in range(B)]
            if g == NG - 1:
                a = [(g, h, b) for b in range(B) for h in (g * GH, g * GH + 1)]
            units += a
        last = None
        project_v(0)
        pending_out = []
        for n, (g, h, b) in enumerate(units):
            idx = n % (GH * B)
            project(h, b, 0)
            project(h, b, 1)
            if idx == 0:
                prefetch_head(g * GH + 1)
            if idx == 2 and g + 1 < NG:
                prefetch_head((g + 1) * GH)
            if last is not None:
                attend(last[1], last[2])
            if idx == 0 and g > 0:
                project_v(g)
            project(h, b, 2)
            scores(h, b)
            if idx == 0 and g > 0:
                out_product(g - 1, 0)
                out_product(g - 1, 1)
            if idx == 1:
                prefetch_o(g)
            if idx == 3 and g + 1 < NG:
                prefetch_v(g + 1)
            last = (g, h, b)
        attend(last[1], last[2])
        for b in range(B):
            out_product(NG - 1, b)
        ffn_ready = load_ffn_weights()
        for b in range(B):
            quantise_ctx(b)
            t_scratch = []
            for s in range(ST):
                t_s, t_x2 = rows_tail(b, s)
                t_scratch.append(t_s)
            ctx_done[0] = t_x2
            t_all = ffn_tail(b, t_scratch, t_x2, ffn_ready)
        PL.wait(t_all)


def kernel(x, ctx_4096, L0_attn_qkv_w, L0_attn_out_w, L0_attn_gate_w, L0_attn_norm_w, L0_xattn_x1_scale,
           L0_xattn_x1_zp, L0_xattn_x2_scale, L0_xattn_x2_zp, L0_ffn_up, L0_ffn_down, L0_ffn_perm):
    import numpy as np
    import concourse.bacc as bacc
    from concourse.bass_utils import run_bass_kernel_spmd

    def rows(a):
        return np.ascontiguousarray(a)

    x = np.asarray(x)
    xf = x.reshape(B * S, D)
    qkv = np.asarray(L0_attn_qkv_w).reshape(H, 3, HD, KT, P)
    slope = (2.0 ** (-8.0 / H * (np.arange(H) + 1.0))) * (1.0 - LAYER_IDX / (N_LAYERS - 1 + 1e-5) + 1e-5)
    dist = np.arange(S)[None, :] - np.arange(P)[:, None]
    decay = np.where(dist >= 0, np.exp(-slope[:, None, None] * np.maximum(dist, 0)), 0.0).astype(np.float32)
    data = {
        "x_t": rows(xf.T.reshape(KT, P, B * S).transpose(1, 0, 2)),
        "x_n": rows(xf.reshape(B, ST, P, D)),
        "w_qk": rows(qkv[:, 0:2].transpose(0, 1, 4, 3, 2).reshape(H, 2, P, KT * HD)),
        "w_v": rows(qkv[:, 2].reshape(NG, GH, HD, KT, P).transpose(0, 4, 3, 1, 2).reshape(NG, P, KT * GH * HD)),
        "w_gate": rows(np.asarray(L0_attn_gate_w).reshape(H, HD, KT, P).transpose(0, 3, 2, 1).reshape(H, P, KT * HD)),
        "w_out": rows(np.asarray(L0_attn_out_w).T.reshape(H, HD, D)),
        "norm_w": rows(np.asarray(L0_attn_norm_w).reshape(H, HD).T),
        "decay": decay,
        "ident": np.eye(P, dtype=np.float32),
        "ctx_in": rows(np.asarray(ctx_4096).reshape(B, KT, P, D)),
        "quant": rows(np.broadcast_to(np.concatenate([np.asarray(a).reshape(1) for a in (
            L0_xattn_x1_scale, L0_xattn_x1_zp, L0_xattn_x2_scale, L0_xattn_x2_zp)])[None, :], (P, 4))),
        "up": rows(np.asarray(L0_ffn_up).reshape(FP, P, FM).transpose(1, 0, 2).reshape(P, FP * FM)),
        "down": rows(np.asarray(L0_ffn_down).reshape(FH, 2, P, FD).transpose(2, 0, 1, 3).reshape(P, FH * 2 * FD)),
        "perm": rows(np.asarray(L0_ffn_perm).reshape(KT, P).T),
    }
    nc = bacc.Bacc("TRN2", target_bir_lowering=False, num_devices=1)
    args = [nc.dram_tensor(n, a.shape, mybir.dt.from_np(a.dtype), kind="ExternalInput").ap() for n, a in data.items()]
    outs = [nc.dram_tensor(f"out_t{b}", (D, S), F32, kind="ExternalOutput").ap() for b in range(B)]
    scratch = [nc.dram_tensor(f"x2_t{b}", (D, S), F32, kind="Internal").ap() for b in range(B)]
    decoder_program(nc, *args, outs, scratch)
    r = run_bass_kernel_spmd(nc, [data], core_ids=[0])
    return np.stack([r.results[0][f"out_t{b}"].T for b in range(B)])
```

```python
import concourse.bass as bass
from concourse import mybir
from contextlib import ExitStack

F32 = mybir.dt.float32
F16 = mybir.dt.float16
BF16 = mybir.dt.bfloat16
I32 = mybir.dt.int32
ALU = mybir.AluOpType
ACT = mybir.ActivationFunctionType

P = 128
B, S, D = 2, 512, 1024
KT = D // P
ST = S // P
H, HD = 32, 128
GH = 2
NG = H // GH
CTX = 1024
FH, FD, FM = 16, 64, 256
FP = FH * FD // P
HALF = 512
W_SCALE = 64.0
G_SCALE = 1.0 / 16.0
EPS = 1e-5
Q_MAX = 255.0
Q_MID = 128.0
ROUND = 1.5 * 2.0 ** 23
LAYER_IDX, N_LAYERS = 1, 32


class Event:

    def __init__(self, sem):
        self.sem, self.count = sem, 0


class Stream:

    def __init__(self, engine):
        self.engine, self.met = engine, {}

    def wait(self, *tokens):
        for token in tokens:
            if token is None:
                continue
            event, value = token
            if self.met.get(event, 0) < value:
                self.met[event] = value
                self.engine.wait_ge(event.sem, value)

    def do(self, fn, signal=None, by=1):
        ins = fn(self.engine)
        if signal is None:
            return None
        ins.then_inc(signal.sem, by)
        signal.count += by
        return signal, signal.count


HELD = object()


class Banks:

    def __init__(self, banks):
        self.banks, self.free, self.at = list(banks), [None] * len(banks), 0

    def take(self):
        while self.free[self.at] is HELD:
            self.at = (self.at + 1) % len(self.banks)
        i, self.at = self.at, (self.at + 1) % len(self.banks)
        token, self.free[i] = self.free[i], HELD
        return i, self.banks[i], token

    def give(self, i, token):
        self.free[i] = token

    def join(self, other):
        self.banks += other.banks
        self.free += other.free


def decoder_program(nc, x_t, x_n, w_qk, w_v, w_gate, w_out, norm_w, decay, ident, ctx_in, quant, up, down,
                    perm, perm2, out_b, scratch_b):
    stack = ExitStack()
    with stack:
        def sb(name, shape, dt):
            return stack.enter_context(nc.sbuf_tensor(name, shape, dt))

        def event(name):
            return Event(stack.enter_context(nc.semaphore(name)))

        x_hl = [sb(f"x_split{b}", [P, 2, KT, S], F16) for b in range(B)]
        x_2 = [t[:, :, :, :].rearrange("p a k s -> p (a k) s") for t in x_hl]
        acc = [sb(f"acc{b}", [P, ST, D], F32) for b in range(B)]
        x2p = [a[:, :, :].rearrange("p t d -> p (t d)").rearrange("p (k s) -> p k s", k=KT) for a in acc]
        w_head = [sb(f"w_head{i}", [P, 3, 2, KT, P], F16) for i in range(2)]
        w_vg = sb("w_v_group", [P, 2, KT, GH * HD], F16)
        w_og = sb("w_out_group", [P, GH, 2, D], F16)
        x0_flat = x_hl[0][:, :, :, :].rearrange("p a k n -> p (a k n)").bitcast(BF16)
        wv_flat = w_vg[:, :, :, :].rearrange("p a k n -> p (a k n)").bitcast(BF16)
        wh_flat = w_head[0][:, :, :, :, :].rearrange("p c a k n -> p (c a k n)").bitcast(BF16)
        ctx_q = [[x0_flat[:, k * D:(k + 1) * D] for k in range(KT)],
                 [(wv_flat, wh_flat)[k // 4][:, (k % 4) * D:(k % 4 + 1) * D] for k in range(KT)]]
        NSTAGE = 5
        raw = [sb(f"raw{i}", [P, D], F32) for i in range(NSTAGE)]
        decay_sb = [sb(f"decay_sb{i}", [P, S], F32) for i in range(2)]
        q_hl = sb("q_split", [P, 2, S], F16)
        k_hl = sb("k_split", [P, 2, S], F16)
        v_hl = [sb(f"v_split{b}", [P, 2, ST, GH * HD], F16) for b in range(B)]
        sig32 = [sb(f"sig32_{i}", [P, S], F32) for i in range(2)]
        gate32 = [sb(f"gate32_{i}", [P, S], F32) for i in range(2)]
        off = {0: 0, 1: S, 3: 2 * S - P, 2: 2 * S}
        NS = sum(S - P * j for j in range(ST))
        s_hl = sb("scores_split", [P, 2, NS], F16)
        g_hl = [sb(f"gated_split{b}", [P, GH, 2, S], F16) for b in range(B)]
        sq32 = sb("square32", [P, S], F32)
        ssq = sb("ssq", [P, B, S], F32)
        nw_sb = sb("norm_w_sb", [P, H], F32)
        ident32 = sb("ident32", [P, P], F32)
        ident16 = sb("ident16", [P, P], BF16)
        ones32 = sb("ones32", [P, P], F32)
        ones16 = sb("ones16", [P, P], BF16)
        perm_sb = sb("perm_sb", [P, KT], I32)
        perm2_sb = sb("perm2_sb", [P, FH], I32)
        quant_sb = sb("quant_sb", [P, 4], F32)
        qc = sb("quant_consts", [P, 12], F32)
        eps_sb = sb("eps_sb", [P, 2], F32)
        up_2 = sb("up_twice", [P, 2, FH, FM], F16)
        down_hl = sb("down_split", [P, 2, FH * 2, FD], F16)
        w1_flat = w_head[1][:, :, :, :, :].rearrange("p c a k n -> p (c a k n)").bitcast(F32)
        NODD = w1_flat.shape[1] // S
        x2odd = [w1_flat[:, i * S:(i + 1) * S] for i in range(NODD)]
        q1_n = [sb(f"q1_n{i}", [P, D], BF16) for i in range(2)]
        q1_t = [sb(f"q1_t{i}", [P, KT, P], BF16) for i in range(2)]
        ctx_row = sb("ctx_row", [P, D], F32)
        stats = [sb(f"stats{s}", [P, 2, 6], F32) for s in range(ST)]
        small = [sb(f"small{s}", [P, 16], F32) for s in range(ST)]
        sum1, sum2, sqf = sig32[0], sig32[1], sq32
        lnc = sb("last_norm_cols", [P, 6, ST], F32)
        diag = [decay_sb[0][:, i * P:(i + 1) * P] for i in range(ST)]
        h_hl = ([v_hl[0][:, :, :, :].rearrange("p a s n -> p (a s n)")[:, i * 2 * S:(i + 1) * 2 * S]
                 .rearrange("p (a s) -> p a s", a=2) for i in range(2)]
                + [g_hl[0][:, i] for i in range(GH)])

        banks = [stack.enter_context(nc.psum_tensor(f"bank{i}", [P, HALF], F32)) for i in range(8)]
        ring = Banks(banks[0:4])
        sring = Banks(banks[4:7])
        aring = Banks(banks[7:8])

        x_in = [[event(f"x_in{b}_{i}") for i in range(KT // 2)] for b in range(B)]
        raw_in = [event(f"raw_in{i}") for i in range(NSTAGE)]
        decay_in = [event(f"decay_in{i}") for i in range(2)]
        const_in = event("const_in")
        pe = event("pe_done")
        act = event("act_done")
        dve = event("dve_done")
        pool = event("pool_done")
        raw_out = [event(f"raw_out{i}") for i in range(NSTAGE)]
        gathered = [[event(f"gathered{b}_{h}") for h in range(FH)] for b in range(B)]
        stored = event("stored")

        SP, PE, AC, DV, PL = (Stream(e) for e in (nc.sync, nc.tensor, nc.scalar, nc.vector, nc.gpsimd))

        raw_free = [None] * NSTAGE
        raw_at = [0]

        def load(src, n=D, queue=SP):
            i = raw_at[0] % NSTAGE
            raw_at[0] += 1
            assert raw_free[i] is not HELD
            SP.wait(*(raw_free[i] or ()))
            raw_free[i] = HELD
            t = SP.do(lambda e: e.dma_start(raw[i][:, 0:n], src), raw_in[i], 16)
            return i, t

        def split(src, n, scale, hi, lo, ready, dst_free, shape=None):
            view = src if shape is None else shape(src)
            AC.wait(*ready, *dst_free)
            t_hi = AC.do(lambda e: e.activation(hi, view, ACT.Copy, scale=scale), act)
            DV.wait(*ready, t_hi)
            t_lo = DV.do(lambda e: e.scalar_tensor_tensor(out=lo, in0=view, scalar=scale, in1=hi,
                                                          op0=ALU.mult, op1=ALU.subtract), dve)
            return t_hi, t_lo

        def load_split(src, n, scale, hi, lo, dst_free=()):
            i, t = load(src, n)
            t_hi, t_lo = split(raw[i][:, 0:n], n, scale, hi, lo, [t], dst_free)
            raw_free[i] = (t_lo,)
            return t_lo

        for dst, src in ((nw_sb, norm_w), (ident32, ident), (perm_sb, perm), (perm2_sb, perm2), (quant_sb, quant)):
            t_const = SP.do(lambda e, dst=dst, src=src: e.dma_start(dst[:, :], src), const_in, 16)
        DV.do(lambda e: e.memset(ones32[:, :], 1.0), dve)
        DV.do(lambda e: e.memset(ones16[:, :], 1.0), dve)
        DV.do(lambda e: e.memset(eps_sb[:, 0:1], EPS), dve)
        DV.do(lambda e: e.memset(eps_sb[:, 1:2], EPS / (G_SCALE * W_SCALE) ** -2), dve)
        t_ones = DV.do(lambda e: e.memset(ssq[:, :, :], 0.0), dve)
        DV.wait(t_const)
        t_ident = DV.do(lambda e: e.tensor_copy(ident16[:, :], ident32[:, :]), dve)
        (S1, Z1, S2, Z2) = (quant_sb[:, i:i + 1] for i in range(4))
        INV1, INV2, C1, C2, S12, C1S, C2S, KC = (qc[:, i:i + 1] for i in range(8))

        def dchain(fn):
            t = DV.do(fn, dve)
            DV.wait(t)
            return t

        DV.wait(t_ident)
        dchain(lambda e: e.reciprocal(INV1, S1))
        dchain(lambda e: e.reciprocal(INV2, S2))
        dchain(lambda e: e.tensor_scalar(C1, Z1, -1.0, Q_MID, ALU.mult, ALU.add))
        dchain(lambda e: e.tensor_scalar(C2, Z2, -1.0, Q_MID, ALU.mult, ALU.add))
        dchain(lambda e: e.tensor_tensor(S12, S1, S2, ALU.mult))
        dchain(lambda e: e.tensor_tensor(C1S, C1, S12, ALU.mult))
        dchain(lambda e: e.tensor_tensor(C2S, C2, S12, ALU.mult))
        dchain(lambda e: e.tensor_tensor(KC, C1S, C2, ALU.mult))
        t_qc = dchain(lambda e: e.tensor_scalar(KC, KC, float(CTX), None, ALU.mult))

        head_ready, head_free = {}, {0: (), 1: ()}
        v_ready, v_free = [()], [()]
        o_ready, o_free = [()], [()]
        decay_ready, decay_free = {}, {0: (), 1: ()}

        def prefetch_head(h):
            slot = h % 2
            wt = w_head[slot]
            tokens = []
            SP.wait(*decay_free[slot])
            decay_ready[slot] = SP.do(lambda e: e.dma_start(decay_sb[slot][:, :], decay[h]), decay_in[slot], 16)
            for c, src in ((0, w_qk[h, 0]), (1, w_qk[h, 1]), (2, w_gate[h])):
                hi = wt[:, c, 0].rearrange("p k m -> p (k m)")
                lo = wt[:, c, 1].rearrange("p k m -> p (k m)")
                tokens.append(load_split(src, D, W_SCALE, hi, lo, head_free[slot]))
                head_ready[slot] = tuple(tokens)
                yield

        def prefetch_v(g):
            half = KT // 2
            tokens = []
            for i in range(2):
                src = w_v[g, :, i * half * GH * HD:(i + 1) * half * GH * HD]
                hi = w_vg[:, 0, i * half:(i + 1) * half].rearrange("p k m -> p (k m)")
                lo = w_vg[:, 1, i * half:(i + 1) * half].rearrange("p k m -> p (k m)")
                tokens.append(load_split(src, D, W_SCALE, hi, lo, v_free[0]))
                v_ready[0] = tuple(tokens)
                yield

        def prefetch_o(g):
            tokens = []
            for i in range(GH):
                tokens.append(load_split(w_out[g * GH + i], D, W_SCALE, w_og[:, i, 0, :], w_og[:, i, 1, :], o_free[0]))
                o_ready[0] = tuple(tokens)
                yield

        def three(out, pairs, ready=None):
            n = 3 * len(pairs)
            m = 0
            for i, ((a_hi, a_lo), (b_hi, b_lo)) in enumerate(pairs):
                if ready:
                    PE.wait(ready[i])
                for a, b_ in ((a_hi, b_hi), (a_hi, b_lo), (a_lo, b_hi)):
                    m += 1
                    t = PE.do(lambda e: e.matmul(out, a, b_, start=m == 1, stop=m == n), pe if m == n else None)
            return t

        sig_at = [0]
        sig_free = [(), ()]

        def silu_split(bank, t_mm, n, hi, lo, dst_free):
            gi = sig_at[0] % 2
            sig_at[0] += 1
            ps, g_ = bank[:, 0:n], sig32[gi][:, 0:n]
            AC.wait(t_mm, *sig_free[gi])
            t_sig = AC.do(lambda e: e.activation(g_, ps, ACT.Sigmoid, scale=1.0 / W_SCALE), act)
            DV.wait(t_sig)
            t_s = DV.do(lambda e: e.scalar_tensor_tensor(out=ps, in0=ps, scalar=1.0 / W_SCALE, in1=g_,
                                                         op0=ALU.mult, op1=ALU.mult), dve)
            sig_free[gi] = (t_s,)
            return split(ps, n, 1.0, hi, lo, [t_s], dst_free)

        x_ready = [[], []]

        def load_x(b):
            for i in range(KT // 2):
                ks = slice(2 * i, 2 * i + 2)
                t = SP.do(lambda e: e.dma_start(x2p[b][:, ks, :], x_t[:, ks, b * S:(b + 1) * S]), x_in[b][i], 16)
                for k in (2 * i, 2 * i + 1):
                    _, t_lo = split(x2p[b][:, k, :], S, 1.0, x_hl[b][:, 0, k], x_hl[b][:, 1, k], [t], ())
                    x_ready[b].append(t_lo)

        qk_ready, qk_free = [None, None], [()]
        gate_ready, gate_free = {}, [(), ()]
        v_done, v_hl_free = [(), ()], [(), ()]
        s_ready, s_free = [()], [()]
        g_done, g_free = {}, [(), ()]
        sq_free, ssq_done, acc_done = [()], [t_ones], {}
        x_last_read = [None, None]

        def project(h, b, c):
            i, bank, free = ring.take()
            PE.wait(free, *head_ready[h % 2])
            wt = w_head[h % 2]
            t = three(bank[:, :], [((wt[:, c, 0, k], wt[:, c, 1, k]), (x_hl[b][:, 0, k], x_hl[b][:, 1, k]))
                                   for k in range(KT)], x_ready[b])
            if c == 2:
                slot = h % 2
                g_ = gate32[slot]
                AC.wait(t, *gate_free[slot])
                t_g = AC.do(lambda e: e.activation(g_[:, :], bank[:, :], ACT.Sigmoid, scale=1.0 / W_SCALE), act)
                gate_ready[(h, b)] = (slot, t_g)
                ring.give(i, t_g)
                head_free[h % 2] = (t,)
                x_last_read[b] = t
            else:
                dst = (q_hl, k_hl)[c]
                ready = silu_split(bank, t, S, dst[:, 0], dst[:, 1], qk_free[0])
                ring.give(i, ready[1])
                qk_ready[c] = ready

        def project_v(b, s):
            i, bank, free = ring.take()
            PE.wait(free, *v_ready[0])
            cols = slice(s * P, (s + 1) * P)
            t = three(bank[:, 0:GH * HD],
                      [((x_hl[b][:, 0, k, cols], x_hl[b][:, 1, k, cols]), (w_vg[:, 0, k], w_vg[:, 1, k]))
                       for k in range(KT)], x_ready[b])
            v_done[b] = silu_split(bank, t, GH * HD, v_hl[b][:, 0, s], v_hl[b][:, 1, s], v_hl_free[b])
            ring.give(i, v_done[b][1])
            v_free[0] = (t,)

        def scores(h, b):
            slot = h % 2
            PE.wait(*qk_ready[0], *qk_ready[1])
            for group in ((0,), (1, 3), (2,)):
                i, bank, free = sring.take()
                PE.wait(free)
                width = 0
                for j in group:
                    n = S - P * j
                    cols, keys = slice(j * P, S), slice(j * P, (j + 1) * P)
                    t = three(bank[:, width:width + n],
                              [((k_hl[:, 0, keys], k_hl[:, 1, keys]), (q_hl[:, 0, cols], q_hl[:, 1, cols]))])
                    width += n
                DV.wait(t, decay_ready[slot])
                width = 0
                for j in group:
                    n = S - P * j
                    ps = bank[:, width:width + n]
                    t_d = DV.do(lambda e: e.tensor_tensor(ps, ps, decay_sb[slot][:, 0:n], ALU.mult), dve)
                    width += n
                start = off[group[0]]
                s_ready[0] = split(bank[:, 0:width], width, 1.0, s_hl[:, 0, start:start + width],
                                   s_hl[:, 1, start:start + width], [t_d], s_free[0])
                sring.give(i, s_ready[0][1])
            qk_free[0] = (t,)
            decay_free[slot] = (t_d,)

        def attend(h, b):
            hh = h % GH
            i, bank, free = aring.take()
            PE.wait(free, *s_ready[0], *v_done[b])
            n_mm = 3 * ST
            m = 0
            for j in range(ST):
                n = S - P * j
                cols, at = slice(hh * HD, (hh + 1) * HD), slice(off[j], off[j] + n)
                vh, vl = v_hl[b][:, 0, j, cols], v_hl[b][:, 1, j, cols]
                sh, sl = s_hl[:, 0, at], s_hl[:, 1, at]
                for a, b_ in ((vh, sh), (vh, sl), (vl, sh)):
                    m += 1
                    t = PE.do(lambda e: e.matmul(bank[:, j * P:S], a, b_, start=m == 1, stop=m == n_mm),
                              pe if m == n_mm else None)
            s_free[0] = (t,)
            v_hl_free[b] = (t,)
            slot, t_gate = gate_ready.pop((h, b))
            AC.wait(t, *sq_free[0])
            t_sq = AC.do(lambda e: e.activation(sq32[:, :], bank[:, :], ACT.Square), act)
            DV.wait(t_sq, t_gate)
            t_g = DV.do(lambda e: e.scalar_tensor_tensor(out=bank[:, :], in0=bank[:, :], scalar=nw_sb[:, h:h + 1],
                                                         in1=gate32[slot][:, :], op0=ALU.mult, op1=ALU.mult), dve)
            gate_free[slot] = (t_g,)
            ready = split(bank[:, :], S, G_SCALE, g_hl[b][:, hh, 0], g_hl[b][:, hh, 1], [t_g], g_free[b])
            aring.give(i, ready[1])
            g_done[(hh, b)] = ready
            DV.wait(ssq_done[0])
            ssq_done[0] = DV.do(lambda e: e.tensor_tensor(ssq[:, b], ssq[:, b], sq32[:, :], ALU.add), dve)
            sq_free[0] = (ssq_done[0],)

        def out_product(g, b, s):
            for half in range(2):
                i, bank, free = ring.take()
                PE.wait(free, *o_ready[0], *(t for hh in range(GH) for t in g_done[(hh, b)]))
                cols, outs = slice(s * P, (s + 1) * P), slice(half * HALF, (half + 1) * HALF)
                t = three(bank[:, :], [((g_hl[b][:, hh, 0, cols], g_hl[b][:, hh, 1, cols]),
                                        (w_og[:, hh, 0, outs], w_og[:, hh, 1, outs])) for hh in range(GH)])
                dst = acc[b][:, s, outs]
                DV.wait(t)
                if g == 0:
                    t_acc = DV.do(lambda e: e.tensor_copy(dst, bank[:, :]), dve)
                else:
                    DV.wait(acc_done[(b, s, half)])
                    t_acc = DV.do(lambda e: e.tensor_tensor(dst, dst, bank[:, :], ALU.add), dve)
                acc_done[(b, s, half)] = t_acc
                ring.give(i, t_acc)
            g_free[b] = (t,)
            o_free[0] = (t,)

        ffn_w_ready = []

        def load_ffn_weights():
            for i in range(FH * FM // D):
                sl = slice(i * D, (i + 1) * D)
                hi = up_2[:, 0].rearrange("p a m -> p (a m)")[:, sl]
                lo = up_2[:, 1].rearrange("p a m -> p (a m)")[:, sl]
                ffn_w_ready.append(load_split(up[:, sl], D, 1.0, hi, lo))
                yield
            n = FH * FD
            for i in range(2):
                sl = slice(i * n, (i + 1) * n)
                hi = down_hl[:, 0].rearrange("p a m -> p (a m)")[:, sl]
                lo = down_hl[:, 1].rearrange("p a m -> p (a m)")[:, sl]
                ffn_w_ready.append(load_split(down[:, sl], n, 1.0, hi, lo))
                yield

        ctx_done = [[], []]
        row_done, row_free = [None], [()]

        def quantise_ctx(b, ks, free):
            for k in ks:
                i, t = load(ctx_in[b, k])
                src = raw[i][:, :]
                DV.wait(t, t_qc)
                t = DV.do(lambda e: e.tensor_scalar(src, src, INV2, Z2, ALU.mult, ALU.add), dve)
                DV.wait(t)
                t = DV.do(lambda e: e.tensor_scalar(src, src, 0.0, Q_MAX, ALU.max, ALU.min), dve)
                DV.wait(t, *free)
                t = DV.do(lambda e: e.tensor_scalar(ctx_q[b][k], src, ROUND, ROUND + Q_MID, ALU.add, ALU.subtract), dve)
                raw_free[i] = (t,)
                ctx_done[b].append(t)
                yield

        def context_row(b):
            for half in range(2):
                outs = slice(half * HALF, (half + 1) * HALF)
                i, bank, free = ring.take()
                PE.wait(free, t_ident, ctx_done[b][-1])
                for k in range(KT):
                    t = PE.do(lambda e: e.matmul(bank[:, :], ones16[:, :], ctx_q[b][k][:, outs], start=k == 0,
                                                 stop=k == KT - 1), pe if k == KT - 1 else None)
                DV.wait(t, *row_free[0])
                row_done[0] = DV.do(lambda e: e.tensor_scalar(ctx_row[:, outs], bank[:, :], C1S, KC, ALU.mult,
                                                              ALU.add), dve)
                ring.give(i, row_done[0])

        def norm_tile(s, x_, ready):
            sm, st = small[s], stats[s]
            DV.wait(*ready)
            for i in range(2):
                t = DV.do(lambda e: e.bn_stats(out=st[:, i, :], in_=x_[:, i * HALF:(i + 1) * HALF]), dve)
            DV.wait(t)
            t = DV.do(lambda e: e.bn_aggr(out=sm[:, 0:2], in_=st[:, :, :]), dve)
            AC.wait(t)
            t = AC.do(lambda e: e.activation(sm[:, 2:3], sm[:, 1:2], ACT.Sqrt, bias=eps_sb[:, 0:1]), act)
            DV.wait(t)
            t = DV.do(lambda e: e.reciprocal(sm[:, 3:4], sm[:, 2:3]), dve)
            DV.wait(t)
            t = DV.do(lambda e: e.tensor_scalar(sm[:, 7:8], sm[:, 0:1], sm[:, 3:4], -1.0, ALU.mult, ALU.mult), dve)
            AC.wait(t)
            return AC.do(lambda e: e.activation(x_, x_, ACT.Identity, bias=sm[:, 7:8], scale=sm[:, 3:4]), act)

        q1n_free, q1t_free = [(), ()], [(), ()]
        tile = [{} for _ in range(ST)]

        def first_norm(b, s):
            x_, sm = acc[b][:, s, :], small[s]
            i, bank, free = ring.take()
            PE.wait(free, ssq_done[0])
            t = PE.do(lambda e: e.matmul(bank[:, 0:1], ssq[:, b, s * P:(s + 1) * P], ones32[:, 0:1],
                                         start=True, stop=True), pe)
            AC.wait(t)
            t_r = AC.do(lambda e: e.activation(sm[:, 4:5], bank[:, 0:1], ACT.Sqrt, bias=eps_sb[:, 1:2],
                                               scale=(G_SCALE * W_SCALE) ** 2 / (H * HD)), act)
            ring.give(i, t_r)
            DV.wait(t_r)
            t = DV.do(lambda e: e.reciprocal(sm[:, 5:6], sm[:, 4:5]), dve)
            i, t_x = load(x_n[b, s])
            DV.wait(t, t_x, acc_done[(b, s, 0)], acc_done[(b, s, 1)])
            t = DV.do(lambda e: e.scalar_tensor_tensor(out=x_, in0=x_, scalar=sm[:, 5:6], in1=raw[i][:, :],
                                                       op0=ALU.mult, op1=ALU.add), dve)
            t1 = norm_tile(s, x_, [t])
            src = raw[i][:, :]
            AC.wait(t1, t_qc)
            t = AC.do(lambda e: e.activation(src, x_, ACT.Identity, bias=Z1, scale=INV1), act)
            DV.wait(t)
            t = DV.do(lambda e: e.tensor_scalar(src, src, 0.0, Q_MAX, ALU.max, ALU.min), dve)
            DV.wait(t, *q1n_free[s % 2])
            t_q = DV.do(lambda e: e.tensor_scalar(q1_n[s % 2][:, :], src, ROUND, ROUND + Q_MID,
                                                  ALU.add, ALU.subtract), dve)
            raw_free[i] = (t_q,)
            tile[s] = {"x1": t1, "q1": t_q}

        def transpose_q1(b, s):
            i, bank, free = ring.take()
            ps = bank[:, :].bitcast(BF16)
            PE.wait(free, tile[s]["q1"], t_ident)
            for k in range(KT):
                t = PE.do(lambda e: e.transpose(ps[:, k * P:(k + 1) * P], q1_n[s % 2][:, k * P:(k + 1) * P],
                                                ident16[:, :]), pe if k == KT - 1 else None)
            q1n_free[s % 2] = (t,)
            AC.wait(t, *q1t_free[s % 2])
            t = AC.do(lambda e: e.activation(q1_t[s % 2][:, :, :].rearrange("p k s -> p (k s)"), ps, ACT.Copy), act)
            ring.give(i, t)
            tile[s]["q1t"] = t

        def cross(b, s):
            x_, sm, qt = acc[b][:, s, :], small[s], q1_t[s % 2]
            i, bank, free = ring.take()
            PE.wait(free, tile[s]["q1t"], ctx_done[b][-1])
            for k in range(KT):
                t = PE.do(lambda e: e.matmul(bank[:, 0:1], qt[:, k, :], ones16[:, 0:1], start=k == 0,
                                             stop=k == KT - 1), pe if k == KT - 1 else None)
            DV.wait(t)
            t = DV.do(lambda e: e.tensor_scalar(sm[:, 6:7], bank[:, 0:1], C2S, None, ALU.mult), dve)
            ring.give(i, t)
            DV.wait(t, tile[s]["x1"], row_done[0])
            t_x = DV.do(lambda e: e.scalar_tensor_tensor(out=x_, in0=x_, scalar=sm[:, 6:7], in1=ctx_row[:, :],
                                                         op0=ALU.add, op1=ALU.add), dve)
            row_free[0] = (t_x,)
            for half in range(2):
                outs = slice(half * HALF, (half + 1) * HALF)
                i, bank, free = ring.take()
                PE.wait(free)
                for k in range(KT):
                    t_mm = PE.do(lambda e: e.matmul(bank[:, :], qt[:, k, :], ctx_q[b][k][:, outs], start=k == 0,
                                                    stop=k == KT - 1), pe if k == KT - 1 else None)
                DV.wait(t_mm, t_x)
                t = DV.do(lambda e: e.scalar_tensor_tensor(out=x_[:, outs], in0=bank[:, :], scalar=S12,
                                                           in1=x_[:, outs], op0=ALU.mult, op1=ALU.add), dve)
                ring.give(i, t)
            q1t_free[s % 2] = (t_mm,)
            tile[s]["x2"] = norm_tile(s, x_, [t])

        x2_stored, x2_read, ctx_read = [[], []], [None, None], [None, None]

        def store_x2(b, s):
            slot = raw_at[0] % NSTAGE
            raw_at[0] += 1
            assert raw_free[slot] is not HELD
            x_ = acc[b][:, s, :]
            for half in range(2):
                i, bank, free = ring.take()
                PE.wait(free, tile[s]["x2"])
                for k in range(4):
                    cols = slice((half * 4 + k) * P, (half * 4 + k + 1) * P)
                    t = PE.do(lambda e: e.transpose(bank[:, k * P:(k + 1) * P], x_[:, cols], ident32[:, :]),
                              pe if k == 3 else None)
                AC.wait(t, *(raw_free[slot] or ()))
                t_c = AC.do(lambda e: e.activation(raw[slot][:, half * HALF:(half + 1) * HALF], bank[:, :],
                                                   ACT.Copy), act)
                ring.give(i, t_c)
            SP.wait(t_c)
            t_s = SP.do(lambda e: e.dma_start(
                scratch_b[b].rearrange("(k p) s -> p k s", p=P)[:, :, s * P:(s + 1) * P],
                raw[slot][:, :].rearrange("p (k s) -> p k s", k=KT)), raw_out[slot], 16)
            raw_free[slot] = (t_s,)
            x2_stored[b].append(t_s)
            x2_read[b] = t

        h_free = [()] * 4
        h_at = [0]
        sum_free = [(), ()]
        sqf_free = [()]
        diag_free, lnc_free = [()], [()]

        def rows_phase(b):
            order = [(first_norm, 0), (first_norm, 1), (transpose_q1, 0), (first_norm, 2), (transpose_q1, 1), (cross, 0),
                     (first_norm, 3), (transpose_q1, 2), (cross, 1), (transpose_q1, 3), (store_x2, 0), (cross, 2),
                     (store_x2, 1), (cross, 3), (store_x2, 2), (store_x2, 3)]
            for step, s in order:
                if (step, s) == (cross, 0):
                    while len(ctx_done[b]) < KT:
                        yield
                    context_row(b)
                    yield
                step(b, s)
                yield
            ctx_read[b] = x2_read[b]

        odd_free = [()] * NODD

        def ffn_phase(b):
            xp = x2p[b]
            got = {}

            def gather(h):
                even = h % 2 == 0
                dst = xp[:, h // 2, :] if even else x2odd[h // 2 % NODD]
                PL.wait(*x2_stored[b], t_const, x2_read[b], *(() if even else odd_free[h // 2 % NODD]))
                got[h] = (dst, PL.do(lambda e: e.indirect_dma_start(
                    dst, None, scratch_b[b], bass.IndirectOffsetOnAxis(ap=perm2_sb[:, h:h + 1], axis=0)),
                    gathered[b][h], 16))

            for h in range(2 * NODD):
                gather(h)
            x_split = {}

            def split_x2(p):
                if p >= FP:
                    return
                x_split[p] = []
                for h in (2 * p, 2 * p + 1):
                    src, t = got[h]
                    dst = x_2[b][:, h, :]
                    AC.wait(t, ctx_read[b])
                    t = AC.do(lambda e: e.activation(dst, src, ACT.Copy), act)
                    DV.wait(t)
                    x_split[p].append(DV.do(lambda e: e.tensor_tensor(dst[FD:P], src[FD:P], dst[FD:P],
                                                                      ALU.subtract), dve))

            hs = {}

            def up_half(p, mc):
                two = [ring.take() for _ in range(2)]
                PE.wait(two[0][2], two[1][2], *x_split[p], *ffn_w_ready)
                for a in range(2):
                    bank, h = two[a][1], 2 * p + a
                    for n in range(2):
                        t = PE.do(lambda e: e.matmul(bank[:, :], up_2[:, n, h, mc * P:(mc + 1) * P], x_2[b][:, h, :],
                                                     start=n == 0, stop=n == 1), pe if n == 1 else None)
                for a in range(2):
                    i, bank, _ = two[a]
                    slot = h_at[0] % 4
                    h_at[0] += 1
                    hi, lo, ps = h_hl[slot][:, 0, :], h_hl[slot][:, 1, :], bank[:, :]
                    AC.wait(t, *h_free[slot])
                    AC.do(lambda e: e.activation(hi, ps, ACT.Gelu), act)
                    t_h = AC.do(lambda e: e.activation(ps, ps, ACT.Gelu), act)
                    DV.wait(t_h)
                    t_lo = DV.do(lambda e: e.tensor_tensor(lo, ps, hi, ALU.subtract), dve)
                    ring.give(i, t_lo)
                    h_free[slot] = HELD
                    hs[(p, a, mc)] = (slot, t_lo)

            ys = {}

            def down_half(p, mc):
                if mc == 0:
                    ys[p] = ring.take()
                i, bank, free = ys[p]
                PE.wait(free)
                for a in range(2):
                    slot, t_h = hs.pop((p, a, mc))
                    PE.wait(t_h)
                    for n, (wi, hi_) in enumerate(((0, 0), (0, 1), (1, 0))):
                        t = PE.do(lambda e: e.matmul(bank[a * FD:(a + 1) * FD, :],
                                                     down_hl[:, wi, (2 * p + a) * 2 + mc, :], h_hl[slot][:, hi_, :],
                                                     start=mc == 0 and n == 0, stop=mc == 1 and n == 2),
                                  pe if n == 2 else None)
                    h_free[slot] = (t,)
                if mc == 1:
                    y, odd = xp[:, p, :], got[2 * p + 1][0]
                    DV.wait(t)
                    DV.do(lambda e: e.tensor_tensor(y[0:FD], bank[0:FD, :], y[0:FD], ALU.add), dve)
                    t = DV.do(lambda e: e.tensor_tensor(y[FD:P], bank[FD:P, :], odd[FD:P], ALU.add), dve)
                    ring.give(i, t)
                    odd_free[p % NODD] = (t,)
                    if p + NODD < FP:
                        gather(2 * (p + NODD))
                        gather(2 * (p + NODD) + 1)
                    AC.wait(t, *sqf_free[0])
                    if p == 0:
                        AC.wait(*sum_free[1])
                        t2 = AC.do(lambda e: e.activation(sum2[:, :], y, ACT.Square), act)
                        PL.wait(t, *sum_free[0])
                        t1 = PL.do(lambda e: e.tensor_copy(sum1[:, :], y), pool)
                    else:
                        t_sq = AC.do(lambda e: e.activation(sqf[:, :], y, ACT.Square), act)
                        PL.wait(t, *sum_free[0])
                        t1 = PL.do(lambda e: e.tensor_tensor(sum1[:, :], sum1[:, :], y, ALU.add), pool)
                        PL.wait(t_sq, *sum_free[1])
                        t2 = PL.do(lambda e: e.tensor_tensor(sum2[:, :], sum2[:, :], sqf[:, :], ALU.add), pool)
                        sqf_free[0] = (t2,)
                    sum_free[0], sum_free[1] = (t1,), (t2,)

            split_x2(0)
            split_x2(1)
            for n in range(2 * FP + 2):
                if n >= 2:
                    down_half((n - 2) // 2, n % 2)
                    yield
                if n < 2 * FP:
                    up_half(n // 2, n % 2)
                    if n % 2:
                        split_x2(n // 2 + 2)
                    yield

            i, bank, free = ring.take()
            PE.wait(free, *sum_free[0], *sum_free[1])
            for s in range(2 * ST):
                src = (sum1, sum2)[s // ST]
                cols = slice(s % ST * P, (s % ST + 1) * P)
                t = PE.do(lambda e: e.matmul(bank[:, s:s + 1], src[:, cols], ones32[:, 0:1], start=True, stop=True),
                          pe if s == 2 * ST - 1 else None)
            sum_free[0] = sum_free[1] = (t,)
            mean, ms, msq, var, sd, rs = (lnc[:, j, :] for j in range(6))
            DV.wait(t, *lnc_free[0])
            DV.do(lambda e: e.tensor_scalar(mean, bank[:, 0:ST], 1.0 / D, None, ALU.mult), dve)
            t = DV.do(lambda e: e.tensor_scalar(ms, bank[:, ST:2 * ST], 1.0 / D, None, ALU.mult), dve)
            ring.give(i, t)
            DV.wait(t)
            t = DV.do(lambda e: e.tensor_tensor(msq, mean, mean, ALU.mult), dve)
            DV.wait(t)
            t = DV.do(lambda e: e.tensor_tensor(var, ms, msq, ALU.subtract), dve)
            AC.wait(t)
            t = AC.do(lambda e: e.activation(sd, var, ACT.Sqrt, bias=eps_sb[:, 0:1]), act)
            DV.wait(t)
            t_rs = DV.do(lambda e: e.reciprocal(rs, sd), dve)
            lnc_free[0] = (t_rs,)
            rows_ = []
            for value, t_v in ((mean, t), (rs, t_rs)):
                i, bank, free = ring.take()
                PE.wait(free)
                for s in range(ST):
                    d = diag[s]
                    DV.wait(t_v, *diag_free[0])
                    t = DV.do(lambda e: e.tensor_scalar(d, ident32[:, :], value[:, s:s + 1], None, ALU.mult), dve)
                    PE.wait(t)
                    t = PE.do(lambda e: e.matmul(bank[:, s * P:(s + 1) * P], ones32[:, :], d, start=True,
                                                 stop=True), pe)
                diag_free[0] = (t,)
                rows_.append((i, bank, t))
            (im, mean_b, t_m), (ir, rstd_b, t_r) = rows_
            DV.wait(t_m)
            for p in range(FP):
                y = xp[:, p, :]
                t = DV.do(lambda e: e.tensor_tensor(y, y, mean_b[:, :], ALU.subtract), dve)
                DV.wait(t, t_r)
                t = DV.do(lambda e: e.tensor_tensor(y, y, rstd_b[:, :], ALU.mult), dve)
                PL.wait(t)
                stores.append(PL.do(lambda e: e.indirect_dma_start(
                    out_b[b], bass.IndirectOffsetOnAxis(ap=perm_sb[:, p:p + 1], axis=0), y, None), stored, 16))
            ring.give(im, t)
            ring.give(ir, t)
            yield

        stores = []

        TAIL_GROUPS = 2
        blocks = [(g, (0, 1)) for g in range(NG - TAIL_GROUPS)]
        blocks += [(g, (b,)) for b in range(B) for g in range(NG - TAIL_GROUPS, NG)]
        idle = []
        tails = []

        def prepare(n=1):
            for _ in range(n):
                while idle:
                    try:
                        next(idle[0])
                        break
                    except StopIteration:
                        idle.pop(0)

        def finish_idle():
            while idle:
                prepare()

        def advance(n=1):
            for _ in range(n):
                if tails:
                    try:
                        next(tails[0])
                    except StopIteration:
                        tails.pop(0)

        load_x(0)
        for _ in prefetch_v(0):
            pass
        for _ in prefetch_head(0):
            pass
        load_x(1)
        extras = []

        def between():
            prepare()
            if extras:
                try:
                    next(extras[0])
                except StopIteration:
                    extras.pop(0)
            advance()

        last = None
        for n, (g, bs) in enumerate(blocks):
            heads = (g * GH, g * GH + 1)
            units = [(h, b) for h in heads for b in bs]
            final = n == len(blocks) - 1
            if n == 0:
                for b in bs:
                    for s in range(ST):
                        project_v(b, s)
            for m, (h, b) in enumerate(units):
                first = m == 0
                finish_idle()
                if first:
                    idle.append(prefetch_head(heads[1]))
                project(h, b, 0)
                between()
                project(h, b, 1)
                between()
                if last is not None:
                    attend(last[1], last[2])
                advance()
                if first and n > 0:
                    for b_ in bs:
                        for s in range(ST):
                            project_v(b_, s)
                            if s % 2:
                                between()
                project(h, b, 2)
                between()
                scores(h, b)
                if first and n > 0:
                    finish_idle()
                    g_, bs_ = blocks[n - 1]
                    for b_ in bs_:
                        for s in range(ST):
                            out_product(g_, b_, s)
                            if s % 2:
                                between()
                    if g_ == NG - 1:
                        h_free[0] = h_free[1] = v_hl_free[0]
                        h_free[2] = h_free[3] = g_free[0]
                        extras += [quantise_ctx(0, range(KT), (x_last_read[0],)), load_ffn_weights()]
                        tails.append(rows_phase(0))
                if h == heads[1] and b == bs[0] and not final:
                    idle.append(prefetch_head(blocks[n + 1][0] * GH))
                if m == 1:
                    idle.append(prefetch_o(g))
                if m == len(units) - 1 and not final:
                    idle.append(prefetch_v(blocks[n + 1][0]))
                if final and m == 0:
                    extras.append(quantise_ctx(1, range(KT), (x_last_read[1], *head_free[0])))
                last = (g, h, b)
        finish_idle()
        while extras or tails:
            between()
        odd_free[:] = [head_free[1]] * NODD
        sum_free[:] = sig_free
        diag_free[0] = decay_free[0]
        ffn0, rows1 = ffn_phase(0), rows_phase(1)
        attend(last[1], last[2])
        sqf_free[0] = sq_free[0]
        ring.join(sring)
        next(ffn0)
        next(ffn0)
        for s in range(ST):
            out_product(NG - 1, 1, s)
            next(ffn0)
        ring.join(aring)
        phases = [(rows1, 1), (ffn0, 2)]
        while phases:
            for phase in list(phases):
                try:
                    for _ in range(phase[1]):
                        next(phase[0])
                except StopIteration:
                    phases.remove(phase)
        for _ in ffn_phase(1):
            pass
        PL.wait(stores[-1])


def kernel(x, ctx_4096, L0_attn_qkv_w, L0_attn_out_w, L0_attn_gate_w, L0_attn_norm_w, L0_xattn_x1_scale,
           L0_xattn_x1_zp, L0_xattn_x2_scale, L0_xattn_x2_zp, L0_ffn_up, L0_ffn_down, L0_ffn_perm):
    import numpy as np
    import concourse.bacc as bacc
    from concourse.bass_utils import run_bass_kernel_spmd

    def rows(a):
        return np.ascontiguousarray(a)

    x = np.asarray(x)
    xf = x.reshape(B * S, D)
    qkv = np.asarray(L0_attn_qkv_w).reshape(H, 3, HD, KT, P)
    slope = (2.0 ** (-8.0 / H * (np.arange(H) + 1.0))) * (1.0 - LAYER_IDX / (N_LAYERS - 1 + 1e-5) + 1e-5)
    dist = np.arange(S)[None, :] - np.arange(P)[:, None]
    decay = np.where(dist >= 0, np.exp(-slope[:, None, None] * np.maximum(dist, 0)), 0.0).astype(np.float32)
    data = {
        "x_t": rows(xf.T.reshape(KT, P, B * S).transpose(1, 0, 2)),
        "x_n": rows(xf.reshape(B, ST, P, D)),
        "w_qk": rows(qkv[:, 0:2].transpose(0, 1, 4, 3, 2).reshape(H, 2, P, KT * HD)),
        "w_v": rows(qkv[:, 2].reshape(NG, GH, HD, KT, P).transpose(0, 4, 3, 1, 2).reshape(NG, P, KT * GH * HD)),
        "w_gate": rows(np.asarray(L0_attn_gate_w).reshape(H, HD, KT, P).transpose(0, 3, 2, 1).reshape(H, P, KT * HD)),
        "w_out": rows(np.asarray(L0_attn_out_w).T.reshape(H, HD, D)),
        "norm_w": rows(np.asarray(L0_attn_norm_w).reshape(H, HD).T),
        "decay": decay,
        "ident": np.eye(P, dtype=np.float32),
        "ctx_in": rows(np.asarray(ctx_4096).reshape(B, KT, P, D)),
        "quant": rows(np.broadcast_to(np.concatenate([np.asarray(a).reshape(1) for a in (
            L0_xattn_x1_scale, L0_xattn_x1_zp, L0_xattn_x2_scale, L0_xattn_x2_zp)])[None, :], (P, 4))),
        "up": rows(np.tile(np.asarray(L0_ffn_up).transpose(1, 0, 2).reshape(FD, FH * FM), (2, 1))),
        "down": rows(np.asarray(L0_ffn_down).reshape(FH, 2, P, FD).transpose(2, 0, 1, 3).reshape(P, FH * 2 * FD)),
        "perm": rows(np.asarray(L0_ffn_perm).reshape(KT, P).T),
        "perm2": rows(np.tile(np.asarray(L0_ffn_perm).reshape(FH, FD).T, (2, 1))),
    }
    nc = bacc.Bacc("TRN2", target_bir_lowering=False, num_devices=1)
    args = [nc.dram_tensor(n, a.shape, mybir.dt.from_np(a.dtype), kind="ExternalInput").ap() for n, a in data.items()]
    outs = [nc.dram_tensor(f"out_t{b}", (D, S), F32, kind="ExternalOutput").ap() for b in range(B)]
    scratch = [nc.dram_tensor(f"x2_t{b}", (D, S), F32, kind="Internal").ap() for b in range(B)]
    decoder_program(nc, *args, outs, scratch)
    r = run_bass_kernel_spmd(nc, [data], core_ids=[0])
    return np.stack([r.results[0][f"out_t{b}"].T for b in range(B)])
```

```python
import concourse.bass as bass
from concourse import mybir
from contextlib import ExitStack

F32 = mybir.dt.float32
F16 = mybir.dt.float16
BF16 = mybir.dt.bfloat16
I32 = mybir.dt.int32
ALU = mybir.AluOpType
ACT = mybir.ActivationFunctionType

P = 128
B, S, D = 2, 512, 1024
KT = D // P
ST = S // P
H, HD = 32, 128
GH = 2
NG = H // GH
CTX = 1024
FH, FD, FM = 16, 64, 256
FP = FH * FD // P
HALF = 512
W_SCALE = 64.0
G_SCALE = 1.0 / 16.0
EPS = 1e-5
Q_MAX = 255.0
Q_MID = 128.0
ROUND = 1.5 * 2.0 ** 23
LAYER_IDX, N_LAYERS = 1, 32


class Event:

    def __init__(self, sem):
        self.sem, self.count = sem, 0


class Stream:

    def __init__(self, engine):
        self.engine, self.met = engine, {}

    def wait(self, *tokens):
        for token in tokens:
            if token is None:
                continue
            event, value = token
            if self.met.get(event, 0) < value:
                self.met[event] = value
                self.engine.wait_ge(event.sem, value)

    def do(self, fn, signal=None, by=1):
        ins = fn(self.engine)
        if signal is None:
            return None
        ins.then_inc(signal.sem, by)
        signal.count += by
        return signal, signal.count


HELD = object()


class Banks:

    def __init__(self, banks):
        self.banks, self.free, self.at = list(banks), [None] * len(banks), 0

    def take(self):
        while self.free[self.at] is HELD:
            self.at = (self.at + 1) % len(self.banks)
        i, self.at = self.at, (self.at + 1) % len(self.banks)
        token, self.free[i] = self.free[i], HELD
        return i, self.banks[i], token

    def give(self, i, token):
        self.free[i] = token

    def join(self, other):
        self.banks += other.banks
        self.free += other.free


def decoder_program(nc, x_t, x_n, w_qk, w_v, w_gate, w_out, norm_w, decay, ident, ctx_in, quant, up, down,
                    perm, perm2, out_b, scratch_b):
    stack = ExitStack()
    with stack:
        def sb(name, shape, dt):
            return stack.enter_context(nc.sbuf_tensor(name, shape, dt))

        def event(name):
            return Event(stack.enter_context(nc.semaphore(name)))

        x_hl = [sb(f"x_split{b}", [P, 2, KT, S], F16) for b in range(B)]
        x_2 = [t[:, :, :, :].rearrange("p a k s -> p (a k) s") for t in x_hl]
        acc = [sb(f"acc{b}", [P, ST, D], F32) for b in range(B)]
        x2p = [a[:, :, :].rearrange("p t d -> p (t d)").rearrange("p (k s) -> p k s", k=KT) for a in acc]
        w_head = [sb(f"w_head{i}", [P, 3, 2, KT, P], F16) for i in range(2)]
        w_vg = sb("w_v_group", [P, 2, KT, GH * HD], F16)
        w_og = sb("w_out_group", [P, GH, 2, D], F16)
        x0_flat = x_hl[0][:, :, :, :].rearrange("p a k n -> p (a k n)").bitcast(BF16)
        wv_flat = w_vg[:, :, :, :].rearrange("p a k n -> p (a k n)").bitcast(BF16)
        wh_flat = w_head[0][:, :, :, :, :].rearrange("p c a k n -> p (c a k n)").bitcast(BF16)
        ctx_q = [[x0_flat[:, k * D:(k + 1) * D] for k in range(KT)],
                 [(wv_flat, wh_flat)[k // 4][:, (k % 4) * D:(k % 4 + 1) * D] for k in range(KT)]]
        NSTAGE = 5
        raw = [sb(f"raw{i}", [P, D], F32) for i in range(NSTAGE)]
        decay_sb = [sb(f"decay_sb{i}", [P, S], F32) for i in range(2)]
        q_hl = sb("q_split", [P, 2, S], F16)
        k_hl = sb("k_split", [P, 2, S], F16)
        v_hl = [sb(f"v_split{b}", [P, 2, ST, GH * HD], F16) for b in range(B)]
        sig32 = [sb(f"sig32_{i}", [P, S], F32) for i in range(2)]
        gate32 = [sb(f"gate32_{i}", [P, S], F32) for i in range(2)]
        off = {0: 0, 1: S, 3: 2 * S - P, 2: 2 * S}
        NS = sum(S - P * j for j in range(ST))
        s_hl = sb("scores_split", [P, 2, NS], F16)
        g_hl = [sb(f"gated_split{b}", [P, GH, 2, S], F16) for b in range(B)]
        sq32 = sb("square32", [P, S], F32)
        ssq = sb("ssq", [P, B, S], F32)
        nw_sb = sb("norm_w_sb", [P, H], F32)
        ident32 = sb("ident32", [P, P], F32)
        ident16 = sb("ident16", [P, P], BF16)
        ones32 = sb("ones32", [P, P], F32)
        ones16 = sb("ones16", [P, P], BF16)
        perm_sb = sb("perm_sb", [P, KT], I32)
        perm2_sb = sb("perm2_sb", [P, FH], I32)
        quant_sb = sb("quant_sb", [P, 4], F32)
        qc = sb("quant_consts", [P, 8], F32)
        neg_half = sb("neg_half", [P, ST], F32)
        up_2 = sb("up_twice", [P, 2, FH, FM], F16)
        down_hl = sb("down_split", [P, 2, FH * 2, FD], F16)
        w1_flat = w_head[1][:, :, :, :, :].rearrange("p c a k n -> p (c a k n)").bitcast(F32)
        NODD = w1_flat.shape[1] // S
        x2odd = [w1_flat[:, i * S:(i + 1) * S] for i in range(NODD)]
        q1_n = [sb(f"q1_n{i}", [P, D], BF16) for i in range(2)]
        q1_t = [sb(f"q1_t{i}", [P, KT, P], BF16) for i in range(2)]
        ctx_row = sb("ctx_row", [P, D], F32)
        stats = [sb(f"stats{s}", [P, 2, 6], F32) for s in range(ST)]
        small = [sb(f"small{s}", [P, 8], F32) for s in range(ST)]
        sums, sqf, sq_last = (sig32, gate32), sq32, decay_sb
        NLAST = len(sq_last)
        h_hl = ([v_hl[0][:, :, :, :].rearrange("p a s n -> p (a s n)")[:, i * 2 * S:(i + 1) * 2 * S]
                 .rearrange("p (a s) -> p a s", a=2) for i in range(2)]
                + [g_hl[0][:, i] for i in range(GH)]
                + [w_og[:, i // 2, i % 2, :].rearrange("p (a s) -> p a s", a=2) for i in range(2 * GH)])

        banks = [stack.enter_context(nc.psum_tensor(f"bank{i}", [P, HALF], F32)) for i in range(8)]
        ring = Banks(banks[0:4])
        sring = Banks(banks[4:7])
        aring = Banks(banks[7:8])

        x_in = [[event(f"x_in{b}_{i}") for i in range(KT // 2)] for b in range(B)]
        raw_in = [event(f"raw_in{i}") for i in range(NSTAGE)]
        decay_in = [event(f"decay_in{i}") for i in range(2)]
        const_in = event("const_in")
        pe = event("pe_done")
        act = event("act_done")
        dve = event("dve_done")
        pool = event("pool_done")
        raw_out = [event(f"raw_out{i}") for i in range(NSTAGE)]
        gathered = [[event(f"gathered{b}_{h}") for h in range(FH)] for b in range(B)]
        stored = event("stored")

        SP, PE, AC, DV, PL = (Stream(e) for e in (nc.sync, nc.tensor, nc.scalar, nc.vector, nc.gpsimd))

        raw_free = [()] * NSTAGE
        raw_at = [0]

        def take_raw():
            while raw_free[raw_at[0] % NSTAGE] is HELD:
                raw_at[0] += 1
            i = raw_at[0] % NSTAGE
            raw_at[0] += 1
            free, raw_free[i] = raw_free[i], HELD
            return i, free

        def load(src):
            i, free = take_raw()
            SP.wait(*free)
            n = src.shape[-1]
            return i, SP.do(lambda e: e.dma_start(raw[i][:, 0:n], src), raw_in[i], 16)

        def split(src, scale, hi, lo, ready, dst_free):
            AC.wait(*ready, *dst_free)
            t_hi = AC.do(lambda e: e.activation(hi, src, ACT.Copy, scale=scale), act)
            DV.wait(*ready, t_hi)
            t_lo = DV.do(lambda e: e.scalar_tensor_tensor(out=lo, in0=src, scalar=scale, in1=hi,
                                                          op0=ALU.mult, op1=ALU.subtract), dve)
            return t_hi, t_lo

        class Loads:
            AHEAD = 2

            def __init__(self):
                self.items = []

            def append(self, key, src, work):
                self.items.append([key, src, work, None])
                self.start()

            def start(self):
                for item in self.items[:self.AHEAD]:
                    if item[3] is None:
                        item[3] = load(item[1])

            def step(self, n=1):
                for _ in range(min(n, len(self.items))):
                    self.start()
                    _, _, work, (i, t) = self.items.pop(0)
                    raw_free[i] = (work(raw[i], t),)
                    self.start()

            def finish(self, key):
                while any(item[0] == key for item in self.items):
                    self.step()

        for dst, src in ((nw_sb, norm_w), (ident32, ident), (perm_sb, perm), (perm2_sb, perm2), (quant_sb, quant)):
            t_const = AC.do(lambda e: e.dma_start(dst[:, :], src), const_in, 16)
        DV.do(lambda e: e.memset(ones32[:, :], 1.0), dve)
        DV.do(lambda e: e.memset(ones16[:, :], 1.0), dve)
        DV.do(lambda e: e.memset(neg_half[:, :], -0.5), dve)
        t_ones = DV.do(lambda e: e.memset(ssq[:, :, :], 0.0), dve)
        (S1, Z1, S2, Z2) = (quant_sb[:, i:i + 1] for i in range(4))
        INV1, INV2, C1, C2, S12, C1S, C2S, KC = (qc[:, i:i + 1] for i in range(8))

        def constants_of_data():
            DV.wait(t_const)
            t_ident = DV.do(lambda e: e.tensor_copy(ident16[:, :], ident32[:, :]), dve)
            for fn in (lambda e: e.reciprocal(INV1, S1),
                       lambda e: e.reciprocal(INV2, S2),
                       lambda e: e.tensor_scalar(C1, Z1, -1.0, Q_MID, ALU.mult, ALU.add),
                       lambda e: e.tensor_scalar(C2, Z2, -1.0, Q_MID, ALU.mult, ALU.add),
                       lambda e: e.tensor_tensor(S12, S1, S2, ALU.mult),
                       lambda e: e.tensor_tensor(C1S, C1, S12, ALU.mult),
                       lambda e: e.tensor_tensor(C2S, C2, S12, ALU.mult),
                       lambda e: e.tensor_tensor(KC, C1S, C2, ALU.mult),
                       lambda e: e.tensor_scalar(KC, KC, float(CTX), None, ALU.mult)):
                t = DV.do(fn, dve)
                DV.wait(t)
            return t_ident, t

        head_ready, head_free = {}, {0: (), 1: ()}
        v_ready, v_free = [()], [()]
        o_ready, o_free = [()], [()]
        decay_ready, decay_free = {}, {0: (), 1: ()}

        idle = Loads()
        extras = Loads()

        def split_work(scale, hi, lo, free, tokens):
            def work(src, t):
                _, t_lo = split(src[:, 0:hi.shape[-1]], scale, hi, lo, [t], free)
                tokens.append(t_lo)
                return t_lo
            return work

        def prefetch_head(h):
            slot = h % 2
            wt = w_head[slot]
            SP.wait(*decay_free[slot])
            decay_ready[slot] = SP.do(lambda e: e.dma_start(decay_sb[slot][:, :], decay[h]), decay_in[slot], 16)
            head_ready[slot] = []
            for c, src in ((0, w_qk[h, 0]), (1, w_qk[h, 1]), (2, w_gate[h])):
                hi, lo = (wt[:, c, n].rearrange("p k m -> p (k m)") for n in range(2))
                idle.append(("head", h), src, split_work(W_SCALE, hi, lo, head_free[slot], head_ready[slot]))

        def prefetch_v(g):
            half = KT // 2
            v_ready[0] = []
            for i in range(2):
                src = w_v[g, :, i * half * GH * HD:(i + 1) * half * GH * HD]
                hi, lo = (w_vg[:, n, i * half:(i + 1) * half].rearrange("p k m -> p (k m)") for n in range(2))
                idle.append(("v", g), src, split_work(W_SCALE, hi, lo, v_free[0], v_ready[0]))

        def prefetch_o(g):
            o_ready[0] = []
            for i in range(GH):
                idle.append(("o", g), w_out[g * GH + i],
                            split_work(W_SCALE, w_og[:, i, 0, :], w_og[:, i, 1, :], o_free[0], o_ready[0]))

        def three(out, pairs, ready=None):
            n = 3 * len(pairs)
            m = 0
            for i, ((a_hi, a_lo), (b_hi, b_lo)) in enumerate(pairs):
                if ready:
                    PE.wait(*ready[i])
                for a, b_ in ((a_hi, b_hi), (a_hi, b_lo), (a_lo, b_hi)):
                    m += 1
                    t = PE.do(lambda e: e.matmul(out, a, b_, start=m == 1, stop=m == n), pe if m == n else None)
            return t

        sig_at = [0]
        sig_free = [(), ()]

        def silu_split(bank, t_mm, n, hi, lo, dst_free):
            gi = sig_at[0] % 2
            sig_at[0] += 1
            ps, g_ = bank[:, 0:n], sig32[gi][:, 0:n]
            AC.wait(t_mm, *sig_free[gi])
            t_sig = AC.do(lambda e: e.activation(g_, ps, ACT.Sigmoid, scale=1.0 / W_SCALE), act)
            DV.wait(t_sig)
            t_s = DV.do(lambda e: e.scalar_tensor_tensor(out=ps, in0=ps, scalar=1.0 / W_SCALE, in1=g_,
                                                         op0=ALU.mult, op1=ALU.mult), dve)
            sig_free[gi] = (t_s,)
            return split(ps, 1.0, hi, lo, [t_s], dst_free)

        x_ready = [[], []]

        def load_x(b, i):
            ks = slice(2 * i, 2 * i + 2)
            t = SP.do(lambda e: e.dma_start(x2p[b][:, ks, :], x_t[:, ks, b * S:(b + 1) * S]), x_in[b][i], 16)
            for k in (2 * i, 2 * i + 1):
                _, t_lo = split(x2p[b][:, k, :], 1.0, x_hl[b][:, 0, k], x_hl[b][:, 1, k], [t], ())
                x_ready[b].append(t_lo)

        qk_ready, qk_free = [None, None], [()]
        gate_ready, gate_free = {}, [(), ()]
        v_done, v_hl_free = [(), ()], [(), ()]
        s_ready, s_free = [()], [()]
        g_done, g_free = {}, [(), ()]
        sq_free, ssq_done, acc_done = [()], [t_ones], {}
        x_last_read = [None, None]

        def project(h, b, c):
            i, bank, free = ring.take()
            PE.wait(free, *head_ready[h % 2])
            wt = w_head[h % 2]
            t = three(bank[:, :], [((wt[:, c, 0, k], wt[:, c, 1, k]), (x_hl[b][:, 0, k], x_hl[b][:, 1, k]))
                                   for k in range(KT)], [(t_x,) for t_x in x_ready[b]])
            if c == 2:
                slot = h % 2
                g_ = gate32[slot]
                AC.wait(t, *gate_free[slot])
                t_g = AC.do(lambda e: e.activation(g_[:, :], bank[:, :], ACT.Sigmoid, scale=1.0 / W_SCALE), act)
                gate_ready[(h, b)] = (slot, t_g)
                ring.give(i, t_g)
                head_free[h % 2] = (t,)
                x_last_read[b] = t
            else:
                dst = (q_hl, k_hl)[c]
                ready = silu_split(bank, t, S, dst[:, 0], dst[:, 1], qk_free[0])
                ring.give(i, ready[1])
                qk_ready[c] = ready

        def project_v(b, s):
            i, bank, free = ring.take()
            PE.wait(free, v_ready[0][0])
            cols = slice(s * P, (s + 1) * P)
            t = three(bank[:, 0:GH * HD],
                      [((x_hl[b][:, 0, k, cols], x_hl[b][:, 1, k, cols]), (w_vg[:, 0, k], w_vg[:, 1, k]))
                       for k in range(KT)],
                      [(x_ready[b][k], v_ready[0][k // (KT // 2)]) for k in range(KT)])
            v_done[b] = silu_split(bank, t, GH * HD, v_hl[b][:, 0, s], v_hl[b][:, 1, s], v_hl_free[b])
            ring.give(i, v_done[b][1])
            v_free[0] = (t,)

        def scores(h, b):
            slot = h % 2
            PE.wait(*qk_ready[0], *qk_ready[1])
            for group in ((0,), (1, 3), (2,)):
                i, bank, free = sring.take()
                PE.wait(free)
                width = 0
                for j in group:
                    n = S - P * j
                    cols, keys = slice(j * P, S), slice(j * P, (j + 1) * P)
                    t = three(bank[:, width:width + n],
                              [((k_hl[:, 0, keys], k_hl[:, 1, keys]), (q_hl[:, 0, cols], q_hl[:, 1, cols]))])
                    width += n
                DV.wait(t, decay_ready[slot])
                width = 0
                for j in group:
                    n = S - P * j
                    ps = bank[:, width:width + n]
                    t_d = DV.do(lambda e: e.tensor_tensor(ps, ps, decay_sb[slot][:, 0:n], ALU.mult), dve)
                    width += n
                start = off[group[0]]
                s_ready[0] = split(bank[:, 0:width], 1.0, s_hl[:, 0, start:start + width],
                                   s_hl[:, 1, start:start + width], [t_d], s_free[0])
                sring.give(i, s_ready[0][1])
            qk_free[0] = (t,)
            decay_free[slot] = (t_d,)

        def attend(h, b):
            hh = h % GH
            i, bank, free = aring.take()
            PE.wait(free, *s_ready[0], *v_done[b])
            n_mm = 3 * ST
            m = 0
            for j in range(ST):
                n = S - P * j
                cols, at = slice(hh * HD, (hh + 1) * HD), slice(off[j], off[j] + n)
                vh, vl = v_hl[b][:, 0, j, cols], v_hl[b][:, 1, j, cols]
                sh, sl = s_hl[:, 0, at], s_hl[:, 1, at]
                for a, b_ in ((vh, sh), (vh, sl), (vl, sh)):
                    m += 1
                    t = PE.do(lambda e: e.matmul(bank[:, j * P:S], a, b_, start=m == 1, stop=m == n_mm),
                              pe if m == n_mm else None)
            s_free[0] = (t,)
            v_hl_free[b] = (t,)
            slot, t_gate = gate_ready.pop((h, b))
            AC.wait(t, *sq_free[0])
            t_sq = AC.do(lambda e: e.activation(sq32[:, :], bank[:, :], ACT.Square), act)
            DV.wait(t_sq, t_gate)
            t_g = DV.do(lambda e: e.scalar_tensor_tensor(out=bank[:, :], in0=bank[:, :], scalar=nw_sb[:, h:h + 1],
                                                         in1=gate32[slot][:, :], op0=ALU.mult, op1=ALU.mult), dve)
            gate_free[slot] = (t_g,)
            ready = split(bank[:, :], G_SCALE, g_hl[b][:, hh, 0], g_hl[b][:, hh, 1], [t_g], g_free[b])
            aring.give(i, ready[1])
            g_done[(hh, b)] = ready
            DV.wait(ssq_done[0])
            ssq_done[0] = DV.do(lambda e: e.tensor_tensor(ssq[:, b], ssq[:, b], sq32[:, :], ALU.add), dve)
            sq_free[0] = (ssq_done[0],)

        def out_product(g, b, s):
            for half in range(2):
                i, bank, free = ring.take()
                PE.wait(free, *o_ready[0], *(t for hh in range(GH) for t in g_done[(hh, b)]))
                cols, outs = slice(s * P, (s + 1) * P), slice(half * HALF, (half + 1) * HALF)
                t = three(bank[:, :], [((g_hl[b][:, hh, 0, cols], g_hl[b][:, hh, 1, cols]),
                                        (w_og[:, hh, 0, outs], w_og[:, hh, 1, outs])) for hh in range(GH)])
                dst = acc[b][:, s, outs]
                DV.wait(t)
                if g == 0:
                    t_acc = DV.do(lambda e: e.tensor_copy(dst, bank[:, :]), dve)
                else:
                    DV.wait(acc_done[(b, s, half)])
                    t_acc = DV.do(lambda e: e.tensor_tensor(dst, dst, bank[:, :], ALU.add), dve)
                acc_done[(b, s, half)] = t_acc
                ring.give(i, t_acc)
            g_free[b] = (t,)
            o_free[0] = (t,)

        ffn_w_ready = []

        def load_ffn_weights():
            for dst, src in ((up_2, up), (down_hl, down)):
                width = dst[:, 0].shape[1] * dst[:, 0].shape[2]
                n = min(width, D)
                for i in range(0, width, n):
                    hi, lo = (dst[:, a].rearrange("p h m -> p (h m)")[:, i:i + n] for a in range(2))
                    extras.append("ffn", src[:, i:i + n], split_work(1.0, hi, lo, (), ffn_w_ready))

        ctx_done = [[], []]
        row_done, row_free = [None], [()]

        def quantise_ctx(b, ks, free):
            def work_on(k):
                def work(src, t):
                    AC.wait(t, t_qc)
                    t = AC.do(lambda e: e.activation(src[:, :], src[:, :], ACT.Identity, bias=Z2, scale=INV2), act)
                    DV.wait(t)
                    t = DV.do(lambda e: e.tensor_scalar(src[:, :], src[:, :], 0.0, Q_MAX, ALU.max, ALU.min), dve)
                    DV.wait(t, *free)
                    t = DV.do(lambda e: e.tensor_scalar(ctx_q[b][k], src[:, :], ROUND, ROUND + Q_MID, ALU.add,
                                                        ALU.subtract), dve)
                    ctx_done[b].append(t)
                    return t
                return work

            for k in ks:
                extras.append("ctx", ctx_in[b, k], work_on(k))

        def context_row(b):
            for half in range(2):
                outs = slice(half * HALF, (half + 1) * HALF)
                i, bank, free = ring.take()
                PE.wait(free, t_ident, ctx_done[b][-1])
                for k in range(KT):
                    t = PE.do(lambda e: e.matmul(bank[:, :], ones16[:, :], ctx_q[b][k][:, outs], start=k == 0,
                                                 stop=k == KT - 1), pe if k == KT - 1 else None)
                DV.wait(t, *row_free[0])
                row_done[0] = DV.do(lambda e: e.tensor_scalar(ctx_row[:, outs], bank[:, :], C1S, KC, ALU.mult,
                                                              ALU.add), dve)
                ring.give(i, row_done[0])

        def rsqrt(out, in_, t):
            PL.wait(t)
            return PL.do(lambda e: e.tensor_tensor(out, in_, neg_half[:, 0:in_.shape[-1]], ALU.pow), pool)

        def norm_tile(s, x_, ready):
            sm, st = small[s], stats[s]
            DV.wait(*ready)
            for i in range(2):
                t = DV.do(lambda e: e.bn_stats(out=st[:, i, :], in_=x_[:, i * HALF:(i + 1) * HALF]), dve)
            DV.wait(t)
            t = DV.do(lambda e: e.bn_aggr(out=sm[:, 0:2], in_=st[:, :, :]), dve)
            PL.wait(t)
            t = PL.do(lambda e: e.tensor_scalar(sm[:, 2:3], sm[:, 1:2], EPS, None, ALU.add), pool)
            t = rsqrt(sm[:, 3:4], sm[:, 2:3], t)
            yield None
            DV.wait(t)
            t = DV.do(lambda e: e.tensor_scalar(sm[:, 7:8], sm[:, 0:1], sm[:, 3:4], -1.0, ALU.mult, ALU.mult), dve)
            AC.wait(t)
            yield AC.do(lambda e: e.activation(x_, x_, ACT.Identity, bias=sm[:, 7:8], scale=sm[:, 3:4]), act)

        q1n_free, q1t_free = [(), ()], [(), ()]

        def rows_tile(b, s):
            x_, sm = acc[b][:, s, :], small[s]
            i, bank, free = ring.take()
            PE.wait(free, ssq_done[0])
            t = PE.do(lambda e: e.matmul(bank[:, 0:1], ssq[:, b, s * P:(s + 1) * P], ones32[:, 0:1],
                                         start=True, stop=True), pe)
            power = (G_SCALE * W_SCALE) ** 2
            DV.wait(t)
            t = DV.do(lambda e: e.tensor_scalar(sm[:, 4:5], bank[:, 0:1], power / (H * HD), power * EPS,
                                                ALU.mult, ALU.add), dve)
            ring.give(i, t)
            t = rsqrt(sm[:, 5:6], sm[:, 4:5], t)
            j, t_x = load(x_n[b, s])
            yield
            DV.wait(t, t_x, acc_done[(b, s, 0)], acc_done[(b, s, 1)])
            t = DV.do(lambda e: e.scalar_tensor_tensor(out=x_, in0=x_, scalar=sm[:, 5:6], in1=raw[j][:, :],
                                                       op0=ALU.mult, op1=ALU.add), dve)
            raw_free[j] = (t,)
            for t_x1 in norm_tile(s, x_, [t]):
                yield
            j, free = take_raw()
            src = raw[j][:, :]
            AC.wait(t_x1, t_qc, *free)
            t = AC.do(lambda e: e.activation(src, x_, ACT.Identity, bias=Z1, scale=INV1), act)
            DV.wait(t)
            t = DV.do(lambda e: e.tensor_scalar(src, src, 0.0, Q_MAX, ALU.max, ALU.min), dve)
            DV.wait(t, *q1n_free[s % 2])
            t = DV.do(lambda e: e.tensor_scalar(q1_n[s % 2][:, :], src, ROUND, ROUND + Q_MID,
                                                ALU.add, ALU.subtract), dve)
            raw_free[j] = (t,)
            yield
            qt = q1_t[s % 2]
            i, bank, free = ring.take()
            ps = bank[:, :].bitcast(BF16)
            PE.wait(free, t, t_ident)
            for k in range(KT):
                t = PE.do(lambda e: e.transpose(ps[:, k * P:(k + 1) * P], q1_n[s % 2][:, k * P:(k + 1) * P],
                                                ident16[:, :]), pe if k == KT - 1 else None)
            q1n_free[s % 2] = (t,)
            AC.wait(t, *q1t_free[s % 2])
            t_q1t = AC.do(lambda e: e.activation(qt[:, :, :].rearrange("p k s -> p (k s)"), ps, ACT.Copy), act)
            ring.give(i, t_q1t)
            yield
            while row_of[0] != b:
                yield
            i, bank, free = ring.take()
            PE.wait(free, t_q1t, ctx_done[b][-1])
            for k in range(KT):
                t = PE.do(lambda e: e.matmul(bank[:, 0:1], qt[:, k, :], ones16[:, 0:1], start=k == 0,
                                             stop=k == KT - 1), pe if k == KT - 1 else None)
            DV.wait(t)
            t = DV.do(lambda e: e.tensor_scalar(sm[:, 6:7], bank[:, 0:1], C2S, None, ALU.mult), dve)
            ring.give(i, t)
            DV.wait(t, t_x1, row_done[0])
            t_x = DV.do(lambda e: e.scalar_tensor_tensor(out=x_, in0=x_, scalar=sm[:, 6:7], in1=ctx_row[:, :],
                                                         op0=ALU.add, op1=ALU.add), dve)
            row_free[0] = (t_x,)
            for half in range(2):
                outs = slice(half * HALF, (half + 1) * HALF)
                i, bank, free = ring.take()
                PE.wait(free)
                for k in range(KT):
                    t_mm = PE.do(lambda e: e.matmul(bank[:, :], qt[:, k, :], ctx_q[b][k][:, outs], start=k == 0,
                                                    stop=k == KT - 1), pe if k == KT - 1 else None)
                DV.wait(t_mm, t_x)
                t = DV.do(lambda e: e.scalar_tensor_tensor(out=x_[:, outs], in0=bank[:, :], scalar=S12,
                                                           in1=x_[:, outs], op0=ALU.mult, op1=ALU.add), dve)
                ring.give(i, t)
            q1t_free[s % 2] = (t_mm,)
            for t_x2 in norm_tile(s, x_, [t]):
                yield
            slot, slot_free = take_raw()
            for half in range(2):
                i, bank, free = ring.take()
                PE.wait(free, t_x2)
                for k in range(4):
                    cols = slice((half * 4 + k) * P, (half * 4 + k + 1) * P)
                    t = PE.do(lambda e: e.transpose(bank[:, k * P:(k + 1) * P], x_[:, cols], ident32[:, :]),
                              pe if k == 3 else None)
                AC.wait(t, *slot_free)
                t_c = AC.do(lambda e: e.activation(raw[slot][:, half * HALF:(half + 1) * HALF], bank[:, :],
                                                   ACT.Copy), act)
                ring.give(i, t_c)
            AC.wait(t_c)
            t_s = AC.do(lambda e: e.dma_start(
                scratch_b[b].rearrange("(k p) s -> p k s", p=P)[:, :, s * P:(s + 1) * P],
                raw[slot][:, :].rearrange("p (k s) -> p k s", k=KT)), raw_out[slot], 16)
            raw_free[slot] = (t_s,)
            x2_stored[b].append(t_s)
            x2_read[b] = t

        x2_stored, x2_read, ctx_read = [[], []], [None, None], [None, None]

        h_free = [()] * 8
        h_at = [0]
        sum_free = [[(), ()] for _ in range(B)]
        sq_last_free = [()] * NLAST
        all_up = [False, False]
        sqf_free = [()]

        row_of = [None]
        STAGGER = (2, 1)

        def rows_phase(b):
            tiles, at = [rows_tile(b, s) for s in range(ST)], 0
            while tiles:
                for s, tile in enumerate(list(tiles)):
                    if at < STAGGER[b] * (s + ST - len(tiles)):
                        continue
                    try:
                        next(tile)
                    except StopIteration:
                        tiles.remove(tile)
                    yield
                at += 1
                if row_of[0] != b and len(ctx_done[b]) == KT and at > 3:
                    context_row(b)
                    row_of[0] = b
                    yield
            ctx_read[b] = x2_read[b]

        odd_free, odd_at, odd_queue = [()] * NODD, [0], []
        got = {}

        def gather(b, h, dst, free):
            PL.wait(*x2_stored[b], t_const, x2_read[b], *free)
            got[(b, h)] = (dst, PL.do(lambda e: e.indirect_dma_start(
                dst, None, scratch_b[b], bass.IndirectOffsetOnAxis(ap=perm2_sb[:, h:h + 1], axis=0)),
                gathered[b][h], 16))

        def odd_of(b, p):
            return (b * FP + p) % NODD

        def gather_odd():
            while odd_queue and odd_free[odd_at[0] % NODD] is not HELD:
                slot = odd_at[0] % NODD
                odd_at[0] += 1
                gather(*odd_queue.pop(0), x2odd[slot], odd_free[slot])
                odd_free[slot] = HELD

        def ffn_phase(b):
            xp = x2p[b]
            odd_queue.extend((b, 2 * p + 1) for p in range(FP))
            for p in range(FP):
                gather(b, 2 * p, xp[:, p, :], ())
                gather_odd()
            yield
            x_split = {}

            def split_x2(p):
                if p >= FP:
                    return
                x_split[p] = []
                for h in (2 * p, 2 * p + 1):
                    src, t = got[(b, h)]
                    dst = x_2[b][:, h, :]
                    AC.wait(t, ctx_read[b])
                    t = AC.do(lambda e: e.activation(dst, src, ACT.Copy), act)
                    DV.wait(t)
                    x_split[p].append(DV.do(lambda e: e.tensor_tensor(dst[FD:P], src[FD:P], dst[FD:P],
                                                                      ALU.subtract), dve))

            hs = {}

            def up_half(p, mc):
                two = [ring.take() for _ in range(2)]
                PE.wait(two[0][2], two[1][2], *x_split[p], *ffn_w_ready)
                for a in range(2):
                    bank, h = two[a][1], 2 * p + a
                    for n in range(2):
                        t = PE.do(lambda e: e.matmul(bank[:, :], up_2[:, n, h, mc * P:(mc + 1) * P], x_2[b][:, h, :],
                                                     start=n == 0, stop=n == 1), pe if n == 1 else None)
                for a in range(2):
                    i, bank, _ = two[a]
                    slot = h_at[0] % len(h_hl)
                    h_at[0] += 1
                    hi, lo, ps = h_hl[slot][:, 0, :], h_hl[slot][:, 1, :], bank[:, :]
                    AC.wait(t, *h_free[slot])
                    AC.do(lambda e: e.activation(hi, ps, ACT.Gelu), act)
                    t_h = AC.do(lambda e: e.activation(ps, ps, ACT.Gelu), act)
                    DV.wait(t_h)
                    t_lo = DV.do(lambda e: e.tensor_tensor(lo, ps, hi, ALU.subtract), dve)
                    ring.give(i, t_lo)
                    h_free[slot] = HELD
                    hs[(p, a, mc)] = (slot, t_lo)

            ys = {}

            def down_half(p, mc):
                if mc == 0:
                    ys[p] = ring.take()
                i, bank, free = ys[p]
                PE.wait(free)
                for a in range(2):
                    slot, t_h = hs.pop((p, a, mc))
                    PE.wait(t_h)
                    for n, (wi, hi_) in enumerate(((0, 0), (0, 1), (1, 0))):
                        t = PE.do(lambda e: e.matmul(bank[a * FD:(a + 1) * FD, :],
                                                     down_hl[:, wi, (2 * p + a) * 2 + mc, :], h_hl[slot][:, hi_, :],
                                                     start=mc == 0 and n == 0, stop=mc == 1 and n == 2),
                                  pe if n == 2 else None)
                    h_free[slot] = (t,)
                if mc == 1:
                    y, odd = xp[:, p, :], got[(b, 2 * p + 1)][0]
                    DV.wait(t)
                    DV.do(lambda e: e.tensor_tensor(y[0:FD], bank[0:FD, :], y[0:FD], ALU.add), dve)
                    t = DV.do(lambda e: e.tensor_tensor(y[FD:P], bank[FD:P, :], odd[FD:P], ALU.add), dve)
                    ring.give(i, t)
                    odd_free[odd_of(b, p)] = (t,)
                    gather_odd()
                    to_sum.append((p, t))

            sum1, sum2 = sums[b]
            to_sum, to_total = [], []
            totals, done, t_y = [], [], {}

            def add_sums():
                if not to_sum:
                    return
                p, t = to_sum.pop(0)
                y = xp[:, p, :]
                free = sum_free[b]
                if p == 0:
                    AC.wait(t, *free[1])
                    t2 = AC.do(lambda e: e.activation(sum2[:, :], y, ACT.Square), act)
                    PL.wait(t, *free[0])
                    t1 = PL.do(lambda e: e.tensor_copy(sum1[:, :], y), pool)
                    free[:] = (t1,), (t2,)
                elif p < FP - NLAST:
                    PL.wait(t, *sqf_free[0])
                    t_sq = PL.do(lambda e: e.tensor_tensor(sqf[:, :], y, y, ALU.mult), pool)
                    PL.wait(*free[0])
                    t1 = PL.do(lambda e: e.tensor_tensor(sum1[:, :], sum1[:, :], y, ALU.add), pool)
                    PL.wait(t_sq, *free[1])
                    t2 = PL.do(lambda e: e.tensor_tensor(sum2[:, :], sum2[:, :], sqf[:, :], ALU.add), pool)
                    sqf_free[0] = (t2,)
                    free[:] = (t1,), (t2,)
                else:
                    i = p - (FP - NLAST)
                    sq = sq_last[i][:, :]
                    AC.wait(t, *sq_last_free[i])
                    t_sq = AC.do(lambda e: e.activation(sq, y, ACT.Square), act)
                    to_total.append((i, y, t, sq, t_sq))

            def total():
                if not to_total:
                    return
                i, y, t_sum, sq, t_sq = to_total.pop(0)
                last_ = i == NLAST - 1
                if i == 0:
                    totals.extend(ring.take() for _ in range(2))
                    PE.wait(*(bank[2] for bank in totals))
                if last_:
                    free = sum_free[b]
                    for (_, bank, _), sum_, t in zip(totals, (sum1, sum2), free):
                        PE.wait(*t)
                        PE.do(lambda e: e.matmul(bank[:, :], ones32[:, :], sum_[:, :], start=i == 0, stop=False))
                for (_, bank, _), src, t in zip(totals, (y, sq), (t_sum, t_sq)):
                    PE.wait(t)
                    t = PE.do(lambda e: e.matmul(bank[:, :], ones32[:, :], src, start=i == 0 and not last_,
                                                 stop=last_), pe)
                    done.append(t)
                sq_last_free[i] = (t,)

            LAG = 3
            split_x2(0)
            split_x2(1)
            yield
            for n in range(2 * FP + LAG):
                if n < 2 * FP:
                    up_half(n // 2, n % 2)
                    if n % 2:
                        split_x2(n // 2 + 2)
                    yield
                all_up[b] = n >= 2 * FP
                add_sums()
                if n >= LAG:
                    down_half((n - LAG) // 2, (n - LAG) % 2)
                    total()
                    yield
            add_sums()
            total()

            (i1, bank1, _), (i2, bank2, _) = totals
            t_s1, t_s2 = done[-2:]
            mean, var, rstd = sum1[:, :], bank2[:, :], sum2[:, :]
            AC.wait(t_s1)
            t_m = AC.do(lambda e: e.activation(mean, bank1[:, :], ACT.Copy, scale=1.0 / D), act)
            AC.wait(t_m)
            ring.give(i1, t_m)
            t = AC.do(lambda e: e.activation(rstd, mean, ACT.Square), act)
            DV.wait(t, t_s2)
            t = DV.do(lambda e: e.scalar_tensor_tensor(out=var, in0=var, scalar=1.0 / D, in1=rstd,
                                                       op0=ALU.mult, op1=ALU.subtract), dve)
            DV.wait(t)
            t = DV.do(lambda e: e.tensor_scalar(var, var, 0.0, EPS, ALU.max, ALU.add), dve)
            DV.wait(t)
            t = DV.do(lambda e: e.reciprocal(rstd, var), dve)
            ring.give(i2, t)
            AC.wait(t)
            t_r = AC.do(lambda e: e.activation(rstd, rstd, ACT.Sqrt), act)
            yield
            BEHIND = 3
            for p in range(FP + BEHIND):
                if p < FP:
                    y = xp[:, p, :]
                    on, event_ = (PL, pool) if b == 0 else (DV, dve)
                    on.wait(t_m)
                    t_y[p] = on.do(lambda e: e.tensor_tensor(y, y, mean, ALU.subtract), event_)
                if p >= BEHIND:
                    done_p = p - BEHIND
                    y = xp[:, done_p, :]
                    DV.wait(t_y[done_p], t_r)
                    t = DV.do(lambda e: e.tensor_tensor(y, y, rstd, ALU.mult), dve)
                    PL.wait(t)
                    stores.append(PL.do(lambda e: e.indirect_dma_start(
                        out_b[b], bass.IndirectOffsetOnAxis(ap=perm_sb[:, done_p:done_p + 1], axis=0), y, None),
                        stored, 16))
                yield

        stores = []

        TAIL_GROUPS = 4
        blocks = [(g, (0, 1)) for g in range(NG - TAIL_GROUPS)]
        blocks += [(g, (b,)) for b in range(B) for g in range(NG - TAIL_GROUPS, NG)]
        tails = []

        prefetch_v(0)
        for i in range(KT // 2):
            if i % 2 == 0:
                idle.step()
            load_x(0, i)
        for i in range(KT // 2):
            load_x(1, i)
        prefetch_head(0)
        idle.finish(("head", 0))
        t_ident, t_qc = constants_of_data()

        def between():
            idle.step(pace)
            extras.step()
            if tails:
                try:
                    next(tails[0])
                except StopIteration:
                    tails.pop(0)

        def run(*phases, until):
            done = set()
            while not until(done):
                for phase, steps in phases:
                    for _ in range(steps):
                        if phase not in done and not until(done):
                            try:
                                next(phase)
                            except StopIteration:
                                done.add(phase)

        last = None
        for n, (g, bs) in enumerate(blocks):
            heads = (g * GH, g * GH + 1)
            units = [(h, b) for h in heads for b in bs]
            final = n == len(blocks) - 1
            if n == NG - TAIL_GROUPS - 1:
                load_ffn_weights()
            pace = (2, 1)[len(bs) - 1]
            if n == 0:
                for b in bs:
                    for s in range(ST):
                        project_v(b, s)
                prefetch_head(heads[1])
                prefetch_o(g)
                prefetch_v(blocks[1][0])
            for m, (h, b) in enumerate(units):
                first = m == 0
                idle.finish(("head", h))
                project(h, b, 0)
                between()
                project(h, b, 1)
                between()
                if last is not None:
                    attend(last[1], last[2])
                if first and n > 0:
                    idle.finish(("v", g))
                    for b_ in bs:
                        for s in range(ST):
                            project_v(b_, s)
                            if s % 2:
                                between()
                    if final:
                        quantise_ctx(1, range(KT // 2), v_free[0])
                    else:
                        prefetch_v(blocks[n + 1][0])
                if first and n > 0 or final:
                    scores(h, b)
                project(h, b, 2)
                between()
                if not final and (not first or n == 0):
                    scores(h, b)
                if first and n > 0:
                    g_, bs_ = blocks[n - 1]
                    idle.finish(("o", g_))
                    for b_ in bs_:
                        for s in range(ST):
                            out_product(g_, b_, s)
                            if s % 2:
                                between()
                    if g_ == NG - 1:
                        h_free[0] = h_free[1] = v_hl_free[0]
                        h_free[2] = h_free[3] = g_free[0]
                        tails.append(rows_phase(0))
                if b == bs[-1] and not final:
                    prefetch_head(blocks[n + 1][0] * GH + h % 2)
                if first and n > 0:
                    prefetch_o(g)
                if g == NG - 1 and (h, b) == (heads[1], 0):
                    quantise_ctx(0, range(KT), (x_last_read[0],))
                if final and first:
                    quantise_ctx(1, range(KT // 2, KT), head_free[0])
                last = (g, h, b)
        while tails:
            between()
        idle.finish(("o", NG - 1))
        odd_free[:] = [head_free[1]] * NODD
        sum_free[0][:] = sig_free
        sq_last_free[:] = decay_free[0], decay_free[1]
        ffn0, rows1 = ffn_phase(0), rows_phase(1)
        next(ffn0)
        attend(last[1], last[2])
        sqf_free[0] = sq_free[0]
        sum_free[1][:] = gate_free
        ring.join(sring)
        next(ffn0)
        for s in range(ST):
            out_product(NG - 1, 1, s)
            extras.step(2)
            if s > 0:
                next(rows1)
        extras.finish("ctx")
        ring.join(aring)
        h_free[4:] = [o_free[0]] * 4
        run((rows1, 4), (ffn0, 1), until=lambda done: rows1 in done)
        ffn1 = ffn_phase(1)
        next(ffn1)
        run((ffn0, 1), until=lambda done: all_up[0])
        run((ffn0, 1), (ffn1, 1), until=lambda done: ffn0 in done)
        run((ffn1, 1), until=lambda done: ffn1 in done)
        PL.wait(stores[-1])


def kernel(x, ctx_4096, L0_attn_qkv_w, L0_attn_out_w, L0_attn_gate_w, L0_attn_norm_w, L0_xattn_x1_scale,
           L0_xattn_x1_zp, L0_xattn_x2_scale, L0_xattn_x2_zp, L0_ffn_up, L0_ffn_down, L0_ffn_perm):
    import numpy as np
    import concourse.bacc as bacc
    from concourse.bass_utils import run_bass_kernel_spmd

    def rows(a):
        return np.ascontiguousarray(a)

    x = np.asarray(x)
    xf = x.reshape(B * S, D)
    qkv = np.asarray(L0_attn_qkv_w).reshape(H, 3, HD, KT, P)
    slope = (2.0 ** (-8.0 / H * (np.arange(H) + 1.0))) * (1.0 - LAYER_IDX / (N_LAYERS - 1 + 1e-5) + 1e-5)
    dist = np.arange(S)[None, :] - np.arange(P)[:, None]
    decay = np.where(dist >= 0, np.exp(-slope[:, None, None] * np.maximum(dist, 0)), 0.0).astype(np.float32)
    data = {
        "x_t": rows(xf.T.reshape(KT, P, B * S).transpose(1, 0, 2)),
        "x_n": rows(xf.reshape(B, ST, P, D)),
        "w_qk": rows(qkv[:, 0:2].transpose(0, 1, 4, 3, 2).reshape(H, 2, P, KT * HD)),
        "w_v": rows(qkv[:, 2].reshape(NG, GH, HD, KT, P).transpose(0, 4, 3, 1, 2).reshape(NG, P, KT * GH * HD)),
        "w_gate": rows(np.asarray(L0_attn_gate_w).reshape(H, HD, KT, P).transpose(0, 3, 2, 1).reshape(H, P, KT * HD)),
        "w_out": rows(np.asarray(L0_attn_out_w).T.reshape(H, HD, D)),
        "norm_w": rows(np.asarray(L0_attn_norm_w).reshape(H, HD).T),
        "decay": decay,
        "ident": np.eye(P, dtype=np.float32),
        "ctx_in": rows(np.asarray(ctx_4096).reshape(B, KT, P, D)),
        "quant": rows(np.broadcast_to(np.concatenate([np.asarray(a).reshape(1) for a in (
            L0_xattn_x1_scale, L0_xattn_x1_zp, L0_xattn_x2_scale, L0_xattn_x2_zp)])[None, :], (P, 4))),
        "up": rows(np.tile(np.asarray(L0_ffn_up).transpose(1, 0, 2).reshape(FD, FH * FM), (2, 1))),
        "down": rows(np.asarray(L0_ffn_down).reshape(FH, 2, P, FD).transpose(2, 0, 1, 3).reshape(P, FH * 2 * FD)),
        "perm": rows(np.asarray(L0_ffn_perm).reshape(KT, P).T),
        "perm2": rows(np.tile(np.asarray(L0_ffn_perm).reshape(FH, FD).T, (2, 1))),
    }
    nc = bacc.Bacc("TRN2", target_bir_lowering=False, num_devices=1)
    args = [nc.dram_tensor(n, a.shape, mybir.dt.from_np(a.dtype), kind="ExternalInput").ap() for n, a in data.items()]
    outs = [nc.dram_tensor(f"out_t{b}", (D, S), F32, kind="ExternalOutput").ap() for b in range(B)]
    scratch = [nc.dram_tensor(f"x2_t{b}", (D, S), F32, kind="Internal").ap() for b in range(B)]
    decoder_program(nc, *args, outs, scratch)
    r = run_bass_kernel_spmd(nc, [data], core_ids=[0])
    return np.stack([r.results[0][f"out_t{b}"].T for b in range(B)])
```
